# Optimizing a Trainium2 kernel written in Bass

```python
import numpy as np
import jax
import jax.numpy as jnp

def _softmax(x, axis=-1):
    return jax.nn.softmax(x, axis=axis)

def _gelu(x):
    return jax.nn.gelu(x, approximate=True)

def _silu(x):
    return jax.nn.silu(x)

def _sigmoid(x):
    return jax.nn.sigmoid(x)

def _layernorm(x, axis=-1, eps=1e-05):
    m = jnp.mean(x, axis=axis, keepdims=True)
    v = jnp.var(x, axis=axis, keepdims=True)
    return (x - m) / jnp.sqrt(v + eps)

def _scatter_add(tgt, idx, src, axis=0):
    return tgt.at[idx].add(src)

def _segment_sum(src, seg, n):
    return jax.ops.segment_sum(src, seg, n)
kernel_name = 'mk_vit_tower_cls_d2_tok_img768_r4_35bd19'

def setup_inputs(seed: int=0):
    np.random.seed(seed)
    _w = jnp.asarray

    def _rec_inputs():
        import jax
        import jax.numpy as jnp
        _rk = jax.random.key(seed)
        x = 7.57192e-06 + 1.00007 * jax.random.normal(jax.random.fold_in(_rk, 1), (32, 3, 224, 224), jnp.float32)
        cls_tok = 0.02 * jax.random.normal(jax.random.fold_in(_rk, 5), (1, 1, 192), jnp.float32)
        return (x, cls_tok)
    x, cls_tok = _rec_inputs()

    def _L0_tok_setup():
        import jax, jax.numpy as jnp
        import numpy as np
        from jax import lax
        P = 16
        S = 8
        key = jax.random.key(seed)
        k1, k2, k3, k4, k5 = jax.random.split(key, 5)
        B, C, H, W = (64, 3, 224, 224)
        D = 192
        patch_dim = C * P * P
        out = (H - P) // S + 1
        n_tok = out * out + 1
        return {'x': jax.random.normal(k1, (B, C, H, W), dtype=jnp.float32), 'w': jax.random.normal(k2, (D, patch_dim), dtype=jnp.float32) * 0.02, 'b': jax.random.normal(k3, (D,), dtype=jnp.float32) * 0.02, 'cls_token': jax.random.normal(k4, (1, 1, D), dtype=jnp.float32), 'pos_embedding': jax.random.normal(k5, (1, n_tok, D), dtype=jnp.float32)}
    _L0_tok_all = _L0_tok_setup()
    _L0_tok_in = {k: v for k, v in _L0_tok_all.items() if k in ('w', 'b', 'cls_token', 'pos_embedding')}
    del _L0_tok_all

    def _L0_attn_setup():
        import jax, jax.numpy as jnp
        import numpy as np
        B, L, D_MODEL = (2, 256, 192)
        D_INNER = 2 * D_MODEL
        N_STATE = 16
        D_CONV = 4
        DT_RANK = max(1, int(np.ceil(D_INNER / 16)))
        EPS_RMS = 1e-05
        LOG_EPS = -7.0
        EXP_CLAMP = 20.0

        def _mamba_block(x, w_norm, w_in, conv_w, conv_b, w_xproj, w_dt, b_dt, A_log, D_param, w_out):
            xn = x * jax.lax.rsqrt(jnp.mean(x * x, axis=-1, keepdims=True) + EPS_RMS) * w_norm
            xz = xn @ w_in
            x_in, z = jnp.split(xz, 2, axis=-1)
            xc = jnp.transpose(x_in, (0, 2, 1))
            k = conv_w[:, None, :]
            yc = jax.lax.conv_general_dilated(xc, k, window_strides=(1,), padding=[(D_CONV - 1, 0)], feature_group_count=D_INNER, dimension_numbers=('NCH', 'OIH', 'NCH'))
            u = jax.nn.silu(jnp.transpose(yc, (0, 2, 1)) + conv_b)
            proj = u @ w_xproj
            dt_i, B_ssm, C_ssm = jnp.split(proj, [DT_RANK, DT_RANK + N_STATE], axis=-1)
            delta = jax.nn.softplus(dt_i @ w_dt + b_dt)
            A = -jnp.exp(A_log)
            log_dA = jnp.clip(delta[..., None] * A[None, None], LOG_EPS, EXP_CLAMP)
            dA = jnp.exp(log_dA)
            dBu = delta[..., None] * B_ssm[:, :, None, :] * u[..., None]
            log_R = jnp.cumsum(jnp.log(jnp.clip(dA, 1e-07)), axis=1)
            R = jnp.exp(jnp.minimum(log_R, EXP_CLAMP))
            S = jnp.cumsum(dBu * jnp.exp(jnp.minimum(-log_R, EXP_CLAMP)), axis=1)
            h = R * S
            y_ssm = jnp.einsum('bln,bldn->bld', C_ssm, h) + u * D_param
            return x + y_ssm * jax.nn.silu(z) @ w_out
        key = jax.random.key(seed)
        ks = jax.random.split(key, 10)
        s = 0.02
        x = jax.random.normal(ks[0], (B, L, D_MODEL), dtype=jnp.float32)
        w_norm = jnp.ones((D_MODEL,), jnp.float32)
        w_in = jax.random.normal(ks[1], (D_MODEL, 2 * D_INNER), jnp.float32) * s
        conv_w = jax.random.normal(ks[2], (D_INNER, D_CONV), jnp.float32) * s
        conv_b = jax.random.normal(ks[3], (D_INNER,), jnp.float32) * s
        w_xproj = jax.random.normal(ks[4], (D_INNER, DT_RANK + 2 * N_STATE), jnp.float32) * s
        w_dt = jax.random.normal(ks[5], (DT_RANK, D_INNER), jnp.float32) * s
        b_dt = jax.random.normal(ks[6], (D_INNER,), jnp.float32) * s
        A_log = jnp.log(jnp.tile(jnp.arange(1, N_STATE + 1, dtype=jnp.float32), (D_INNER, 1)))
        D_param = jnp.ones((D_INNER,), jnp.float32)
        w_out = jax.random.normal(ks[7], (D_INNER, D_MODEL), jnp.float32) * s
        return {'x': x, 'w_norm': w_norm, 'w_in': w_in, 'conv_w': conv_w, 'conv_b': conv_b, 'w_xproj': w_xproj, 'w_dt': w_dt, 'b_dt': b_dt, 'A_log': A_log, 'D_param': D_param, 'w_out': w_out}
    _L0_attn_all = _L0_attn_setup()
    _L0_attn_in = {k: v for k, v in _L0_attn_all.items() if k in ('w_norm', 'w_in', 'conv_w', 'conv_b', 'w_xproj', 'w_dt', 'b_dt', 'A_log', 'D_param', 'w_out')}
    del _L0_attn_all

    def _L0_ffn_setup():
        import jax, jax.numpy as jnp
        import numpy as np
        H = 192
        R = 64
        E = 8
        B, S = (8, 512)
        key = jax.random.key(seed)
        ks = jax.random.split(key, 10)
        s_in = 1.0 / np.sqrt(H)
        s_r = 1.0 / np.sqrt(R)
        return {'x': jax.random.normal(ks[0], (B, S, H), dtype=jnp.float32), 'enc_w': jax.random.uniform(ks[1], (H, R), jnp.float32, -s_in, s_in), 'enc_b': jax.random.uniform(ks[2], (R,), jnp.float32, -s_in, s_in), 'sw_w': jax.random.uniform(ks[3], (R, E), jnp.float32, -s_r, s_r), 'sw_b': jax.random.uniform(ks[4], (E,), jnp.float32, -s_r, s_r), 'w1': jax.random.uniform(ks[5], (E, H, R), jnp.float32, -s_in, s_in), 'b1': jax.random.uniform(ks[6], (E, R), jnp.float32, -s_in, s_in), 'w2': jax.random.uniform(ks[7], (E, R, H), jnp.float32, -s_r, s_r), 'b2': jax.random.uniform(ks[8], (E, H), jnp.float32, -s_r, s_r)}
    _L0_ffn_all = _L0_ffn_setup()
    _L0_ffn_in = {k: v for k, v in _L0_ffn_all.items() if k in ('enc_w', 'enc_b', 'sw_w', 'sw_b', 'w1', 'b1', 'w2', 'b2')}
    del _L0_ffn_all

    def _L1_attn_setup():
        import jax, jax.numpy as jnp
        import numpy as np
        B, N, C, H = (4, 512, 192, 12)
        D = C // H
        SCALE = D ** (-0.5)
        key = jax.random.key(seed)
        k1, k2, k3 = jax.random.split(key, 3)
        x = jax.random.normal(k1, (B, N, C), dtype=jnp.float32)
        w_qkv = jax.random.normal(k2, (C, 3 * C), dtype=jnp.float32) * 0.02
        w_proj = jax.random.normal(k3, (C, C), dtype=jnp.float32) * 0.02
        b_proj = jnp.zeros((C,), dtype=jnp.float32)
        temperature = jnp.ones((H, 1, 1), dtype=jnp.float32) * 0.5
        return {'x': x, 'w_qkv': w_qkv, 'w_proj': w_proj, 'b_proj': b_proj, 'temperature': temperature}
    _L1_attn_all = _L1_attn_setup()
    _L1_attn_in = {k: v for k, v in _L1_attn_all.items() if k in ('w_qkv', 'w_proj', 'b_proj', 'temperature')}
    del _L1_attn_all

    def _L1_ffn_setup():
        import jax, jax.numpy as jnp
        import numpy as np
        DEPTH = 11

        def _fff_forward(inputs, weights_in, weights_out, depth=DEPTH):
            B, S, _ = inputs.shape
            n_nodes = weights_in.shape[0]
            max_index = n_nodes - 1
            all_logits = jnp.einsum('bsd,nd->bsn', inputs, weights_in)

            def step(prev_idx, _):
                sel = jnp.clip(prev_idx, 0, max_index)
                logits = jnp.take_along_axis(all_logits, sel[..., None], axis=-1)[..., 0]
                new_idx = jnp.clip(2 * sel + 1 + (logits > 0).astype(sel.dtype), 0, max_index)
                return (new_idx, (logits, new_idx))
            idx0 = jnp.zeros((B, S), dtype=jnp.int32)
            _, (logits_seq, idx_seq) = jax.lax.scan(step, idx0, None, length=depth - 1)
            logits = jnp.concatenate([jnp.zeros((1, B, S), all_logits.dtype), logits_seq], axis=0)
            node_idx = jnp.concatenate([idx0[None], idx_seq], axis=0)
            act = jax.nn.gelu(logits, approximate=False)
            onehot = jax.nn.one_hot(node_idx, n_nodes, dtype=act.dtype)
            coeff = jnp.einsum('dbs,dbsn->bsn', act, onehot)
            return jnp.einsum('bsn,nd->bsd', coeff, weights_out)
        key = jax.random.key(seed)
        k1, k2, k3 = jax.random.split(key, 3)
        B, S, D = (4, 1024, 192)
        n_nodes = 2 * DEPTH - 1
        return {'inputs': jax.random.normal(k1, (B, S, D), dtype=jnp.float32), 'weights_in': jax.random.normal(k2, (n_nodes, D), dtype=jnp.float32), 'weights_out': jax.random.normal(k3, (n_nodes, D), dtype=jnp.float32)}
    _L1_ffn_all = _L1_ffn_setup()
    _L1_ffn_in = {k: v for k, v in _L1_ffn_all.items() if k in ('weights_in', 'weights_out')}
    del _L1_ffn_all
    return {'x': x, 'cls_tok': cls_tok, 'L0_tok_w': _L0_tok_in['w'], 'L0_tok_b': _L0_tok_in['b'], 'L0_tok_cls_token': _L0_tok_in['cls_token'], 'L0_tok_pos_embedding': _L0_tok_in['pos_embedding'], 'L0_attn_w_norm': _L0_attn_in['w_norm'], 'L0_attn_w_in': _L0_attn_in['w_in'], 'L0_attn_conv_w': _L0_attn_in['conv_w'], 'L0_attn_conv_b': _L0_attn_in['conv_b'], 'L0_attn_w_xproj': _L0_attn_in['w_xproj'], 'L0_attn_w_dt': _L0_attn_in['w_dt'], 'L0_attn_b_dt': _L0_attn_in['b_dt'], 'L0_attn_A_log': _L0_attn_in['A_log'], 'L0_attn_D_param': _L0_attn_in['D_param'], 'L0_attn_w_out': _L0_attn_in['w_out'], 'L0_ffn_enc_w': _L0_ffn_in['enc_w'], 'L0_ffn_enc_b': _L0_ffn_in['enc_b'], 'L0_ffn_sw_w': _L0_ffn_in['sw_w'], 'L0_ffn_sw_b': _L0_ffn_in['sw_b'], 'L0_ffn_w1': _L0_ffn_in['w1'], 'L0_ffn_b1': _L0_ffn_in['b1'], 'L0_ffn_w2': _L0_ffn_in['w2'], 'L0_ffn_b2': _L0_ffn_in['b2'], 'L1_attn_w_qkv': _L1_attn_in['w_qkv'], 'L1_attn_w_proj': _L1_attn_in['w_proj'], 'L1_attn_b_proj': _L1_attn_in['b_proj'], 'L1_attn_temperature': _L1_attn_in['temperature'], 'L1_ffn_weights_in': _L1_ffn_in['weights_in'], 'L1_ffn_weights_out': _L1_ffn_in['weights_out']}

def reference(x, cls_tok, L0_tok_w, L0_tok_b, L0_tok_cls_token, L0_tok_pos_embedding, L0_attn_w_norm, L0_attn_w_in, L0_attn_conv_w, L0_attn_conv_b, L0_attn_w_xproj, L0_attn_w_dt, L0_attn_b_dt, L0_attn_A_log, L0_attn_D_param, L0_attn_w_out, L0_ffn_enc_w, L0_ffn_enc_b, L0_ffn_sw_w, L0_ffn_sw_b, L0_ffn_w1, L0_ffn_b1, L0_ffn_w2, L0_ffn_b2, L1_attn_w_qkv, L1_attn_w_proj, L1_attn_b_proj, L1_attn_temperature, L1_ffn_weights_in, L1_ffn_weights_out):
    import jax
    import jax.numpy as jnp

    def _L0_tok_ref(x, w, b, cls_token, pos_embedding):
        import jax, jax.numpy as jnp
        import numpy as np
        from jax import lax
        P = 16
        S = 8
        B = x.shape[0]
        patches = lax.conv_general_dilated_patches(x, filter_shape=(P, P), window_strides=(S, S), padding='VALID', dimension_numbers=('NCHW', 'OIHW', 'NCHW'))
        pd = patches.shape[1]
        patches = patches.reshape(B, pd, -1).transpose(0, 2, 1)
        tok = jnp.einsum('bnp,dp->bnd', patches, w) + b
        cls = jnp.broadcast_to(cls_token, (B, 1, tok.shape[-1]))
        out = jnp.concatenate([cls, tok], axis=1) + pos_embedding
        return out

    def _L0_attn_ref(x, w_norm, w_in, conv_w, conv_b, w_xproj, w_dt, b_dt, A_log, D_param, w_out):
        import jax, jax.numpy as jnp
        import numpy as np
        B, L, D_MODEL = (2, 256, 192)
        D_INNER = 2 * D_MODEL
        N_STATE = 16
        D_CONV = 4
        DT_RANK = max(1, int(np.ceil(D_INNER / 16)))
        EPS_RMS = 1e-05
        LOG_EPS = -7.0
        EXP_CLAMP = 20.0

        def _mamba_block(x, w_norm, w_in, conv_w, conv_b, w_xproj, w_dt, b_dt, A_log, D_param, w_out):
            xn = x * jax.lax.rsqrt(jnp.mean(x * x, axis=-1, keepdims=True) + EPS_RMS) * w_norm
            xz = xn @ w_in
            x_in, z = jnp.split(xz, 2, axis=-1)
            xc = jnp.transpose(x_in, (0, 2, 1))
            k = conv_w[:, None, :]
            yc = jax.lax.conv_general_dilated(xc, k, window_strides=(1,), padding=[(D_CONV - 1, 0)], feature_group_count=D_INNER, dimension_numbers=('NCH', 'OIH', 'NCH'))
            u = jax.nn.silu(jnp.transpose(yc, (0, 2, 1)) + conv_b)
            proj = u @ w_xproj
            dt_i, B_ssm, C_ssm = jnp.split(proj, [DT_RANK, DT_RANK + N_STATE], axis=-1)
            delta = jax.nn.softplus(dt_i @ w_dt + b_dt)
            A = -jnp.exp(A_log)
            log_dA = jnp.clip(delta[..., None] * A[None, None], LOG_EPS, EXP_CLAMP)
            dA = jnp.exp(log_dA)
            dBu = delta[..., None] * B_ssm[:, :, None, :] * u[..., None]
            log_R = jnp.cumsum(jnp.log(jnp.clip(dA, 1e-07)), axis=1)
            R = jnp.exp(jnp.minimum(log_R, EXP_CLAMP))
            S = jnp.cumsum(dBu * jnp.exp(jnp.minimum(-log_R, EXP_CLAMP)), axis=1)
            h = R * S
            y_ssm = jnp.einsum('bln,bldn->bld', C_ssm, h) + u * D_param
            return x + y_ssm * jax.nn.silu(z) @ w_out
        return _mamba_block(x, w_norm, w_in, conv_w, conv_b, w_xproj, w_dt, b_dt, A_log, D_param, w_out)

    def _L0_ffn_ref(x, enc_w, enc_b, sw_w, sw_b, w1, b1, w2, b2):
        import jax, jax.numpy as jnp
        import numpy as np
        H = 192
        R = 64
        E = 8
        B, S = (8, 512)
        b, s, d = x.shape
        xt = x.reshape(-1, d)
        x_enc = xt @ enc_w + enc_b
        route_prob = jax.nn.softmax(x_enc @ sw_w + sw_b, axis=-1)
        route_prob_max = jnp.max(route_prob, axis=-1)
        routes = jnp.argmax(route_prob, axis=-1)
        onehot = jax.nn.one_hot(routes, E, dtype=xt.dtype)
        h = jnp.einsum('td,edr->ter', xt, w1) + b1[None]
        h = jax.nn.gelu(h, approximate=False)
        h = h * onehot[..., None]
        out = jnp.einsum('ter,erd->td', h, w2) + onehot @ b2
        out = out * route_prob_max[:, None]
        return out.reshape(b, s, d)

    def _L1_attn_ref(x, w_qkv, w_proj, b_proj, temperature):
        import jax, jax.numpy as jnp
        import numpy as np
        B, N, C, H = (4, 512, 192, 12)
        D = C // H
        SCALE = D ** (-0.5)
        b, n, c = x.shape
        h, d = (H, c // H)
        qkv = (x @ w_qkv).reshape(b, n, 3, h, d)
        q, k, v = jnp.moveaxis(qkv, 2, 0)
        q = q.transpose(0, 2, 1, 3)
        k = k.transpose(0, 2, 1, 3)
        v = v.transpose(0, 2, 1, 3)
        attn = jnp.einsum('bhnd,bhmd->bhnm', q, k) * SCALE
        eye = jnp.eye(n, dtype=attn.dtype)
        attn = attn * (1.0 - temperature[None] * eye)
        attn = jax.nn.softmax(attn, axis=-1)
        out = jnp.einsum('bhnm,bhmd->bhnd', attn, v)
        out = out.transpose(0, 2, 1, 3).reshape(b, n, c)
        return out @ w_proj + b_proj

    def _L1_ffn_ref(inputs, weights_in, weights_out):
        import jax, jax.numpy as jnp
        import numpy as np
        DEPTH = 11

        def _fff_forward(inputs, weights_in, weights_out, depth=DEPTH):
            B, S, _ = inputs.shape
            n_nodes = weights_in.shape[0]
            max_index = n_nodes - 1
            all_logits = jnp.einsum('bsd,nd->bsn', inputs, weights_in)

            def step(prev_idx, _):
                sel = jnp.clip(prev_idx, 0, max_index)
                logits = jnp.take_along_axis(all_logits, sel[..., None], axis=-1)[..., 0]
                new_idx = jnp.clip(2 * sel + 1 + (logits > 0).astype(sel.dtype), 0, max_index)
                return (new_idx, (logits, new_idx))
            idx0 = jnp.zeros((B, S), dtype=jnp.int32)
            _, (logits_seq, idx_seq) = jax.lax.scan(step, idx0, None, length=depth - 1)
            logits = jnp.concatenate([jnp.zeros((1, B, S), all_logits.dtype), logits_seq], axis=0)
            node_idx = jnp.concatenate([idx0[None], idx_seq], axis=0)
            act = jax.nn.gelu(logits, approximate=False)
            onehot = jax.nn.one_hot(node_idx, n_nodes, dtype=act.dtype)
            coeff = jnp.einsum('dbs,dbsn->bsn', act, onehot)
            return jnp.einsum('bsn,nd->bsd', coeff, weights_out)
        return _fff_forward(inputs, weights_in, weights_out)
    h = _L0_tok_ref(x, L0_tok_w, L0_tok_b, L0_tok_cls_token, L0_tok_pos_embedding)
    h = jnp.concatenate([jnp.broadcast_to(cls_tok, (h.shape[0], 1, h.shape[2])), h], axis=1)
    h = h + _L0_attn_ref(_layernorm(h, axis=-1), L0_attn_w_norm, L0_attn_w_in, L0_attn_conv_w, L0_attn_conv_b, L0_attn_w_xproj, L0_attn_w_dt, L0_attn_b_dt, L0_attn_A_log, L0_attn_D_param, L0_attn_w_out)
    h = h + _L0_ffn_ref(_layernorm(h, axis=-1), L0_ffn_enc_w, L0_ffn_enc_b, L0_ffn_sw_w, L0_ffn_sw_b, L0_ffn_w1, L0_ffn_b1, L0_ffn_w2, L0_ffn_b2)
    h = h + _L1_attn_ref(_layernorm(h, axis=-1), L1_attn_w_qkv, L1_attn_w_proj, L1_attn_b_proj, L1_attn_temperature)
    h = h + _L1_ffn_ref(_layernorm(h, axis=-1), L1_ffn_weights_in, L1_ffn_weights_out)
    return h

_drawn_inputs = setup_inputs


def setup_inputs(seed=0):
    import zlib

    import numpy as np

    out = dict(_drawn_inputs(seed))
    spreads = {'L0_attn_w_norm': (1.0, 0.6),
     'L0_attn_D_param': (1.0, 0.6),
     'L1_attn_b_proj': (0.0, 0.1),
     'L1_attn_temperature': (0.5, 0.6)}
    factors = {'cls_tok': 3.184,
     'L0_tok_cls_token': 8.0,
     'L0_attn_w_in': 8.0,
     'L0_attn_conv_w': 8.0,
     'L0_attn_conv_b': 8.0,
     'L0_attn_w_xproj': 8.0,
     'L0_attn_w_dt': 8.0,
     'L0_attn_b_dt': 8.0,
     'L0_attn_A_log': 8.0,
     'L0_attn_w_out': 8.0,
     'L0_ffn_enc_b': 22.099,
     'L0_ffn_b1': 20.401,
     'L1_attn_w_qkv': 7.587,
     'L1_attn_w_proj': 5.108,
     'L0_ffn_sw_b': 3.234,
     'L0_ffn_b2': 3.883}
    for name, (base, spread) in spreads.items():
        noise = np.random.default_rng([zlib.crc32(name.encode()), seed]).standard_normal(out[name].shape)
        drawn = base * np.exp(spread * noise) if base else spread * noise
        out[name] = jnp.asarray(drawn.astype(out[name].dtype))
    for name, factor in factors.items():
        out[name] = (out[name] * factor).astype(out[name].dtype)
    return out
```

```python
from contextlib import ExitStack

import numpy as np

import concourse.bass as bass
from concourse import mybir

F32 = mybir.dt.float32
BF16 = mybir.dt.bfloat16
I32 = mybir.dt.int32
ALU = mybir.AluOpType
ACT = mybir.ActivationFunctionType
AX = mybir.AxisListType

B, C, IMG = 32, 3, 224
P, S = 16, 8
NY = IMG // S
OUT = (IMG - P) // S + 1
T = OUT * OUT + 2
D = 192
KD = 96
NT = (T + 127) // 128
LAST = T - 128 * (NT - 1)
TW = NT * 128
CW = (T + 1) // 2
T2 = 2 * CW
DI, ND = 384, 3
NS, RANK = 16, 24
BROW, CROW = 32, 64
LS = 24
NG = NS - 1
E, R = 8, 64
H, DH = 12, 16
DEPTH = 11
NODES = 2 * DEPTH - 1
EPS = 1e-5
BIG = 1e30
CLAMP, LOW = 20.0, -7.0
DEAD = -104.0
HALVES = [(0, 4), (4, 2)]

JOBS = (["emb0", "emb1", "xnT0", "xnT1"]
        + [f"xz{m}" for m in range(6)] + ["proj"] + [f"dt{m}" for m in range(ND)]
        + ["B0", "C0", "BC15", "mix0", "mix1"]
        + ["x2T0", "x2T1", "route", "hotT"] + [f"{k}{m}" for m in range(4) for k in ("hid", "mask")]
        + ["ffn0", "ffn1"]
        + ["x3T0", "x3T1", "q0", "q1", "k0", "k1", "v0", "v1", "self"]
        + [f"S{h}_{j}" for h in range(H) for j in range(NT)] + ["shiftT0", "shiftT1"]
        + [f"ST{h}_{j}" for g in range(3) for j in range(NT) for h in range(4 * g, 4 * g + 4)]
        + ["oT0", "oT1", "oT2", "aoT0", "aoT1", "att0", "att1"]
        + ["x4T0", "x4T1", "tree", "coefT", "out0", "out1"])
SLOTS = 3
SLOT = {name: n % SLOTS for n, name in enumerate(JOBS)}
TURN = {name: n // SLOTS for n, name in enumerate(JOBS)}
TURNS = [sum(s == k for s in SLOT.values()) for k in range(SLOTS)]

COUNTS = dict(
    dve_chain=66, act_chain=3, pool_chain=8,
    pixels_in=16, pixels_sorted=2, front_done=8, front_taken=8,
    stats_ready=4, rstd_ready=4, norm_ready=4, h_summed=2, xn_ready=1, 
    conv_ready=3, u_ready=3, pre_ready=3, soft_ready=3,
    delta_ready=3, du_ready=3, decay_log_ready=3, decays_ready=3, bc_ready=1, log15_ready=1, decays15_ready=1,
    gated_ready=1, end_ready=1, alive_ready=1, hot_ready=1, exp_ready=1, logits_ready=1,
    parts1_ready=4, rest_ready=4, parts2_ready=4, split_ready=4,
    selfprod_ready=2, shift_ready=1, ones_ready=1,
    parts_out=64, stack_in=192, shift_out=32, shift_in=32, pv_done=18, pv_taken=3,
    self_exp=1, ao_ready=3, tree_ready=1, tree_gelu=1, coef_ready=1, 
    out_stored=32,
)


AHEAD = {"pixels_in": 16, "pixels_sorted": 2, "front_done": 8, "front_taken": 8, "out_stored": 1}
PSUM_AHEAD = 1
TAIL_STEPS = 17
COUNTS.update(tail_flag=1, tail_bc=NG, tail_log=ND * NG, tail_exp=ND * NG, tail_used=NG, tail_chain=NG * TAIL_STEPS)


def at(i, name, k):
    return i * COUNTS[name] + (k + AHEAD.get(name, 0))


def vacant(i, job):
    return i * TURNS[SLOT[job]] + (TURN[job] + PSUM_AHEAD)


def filled(i, job):
    return i * TURNS[SLOT[job]] + (TURN[job] + 1)


def freed(i, job):
    return i * TURNS[SLOT[job]] + (TURN[job] + 1 + PSUM_AHEAD)


def tower(nc, ap, out):
    ctx = ExitStack()
    with ctx:
        def sb(name, shape, dt=F32):
            return ctx.enter_context(nc.sbuf_tensor(name, shape, dt))

        dve_chain = ctx.enter_context(nc.semaphore("dve_chain"))
        act_chain = ctx.enter_context(nc.semaphore("act_chain"))
        pool_chain = ctx.enter_context(nc.semaphore("pool_chain"))
        pixels_in = ctx.enter_context(nc.semaphore("pixels_in"))
        pixels_sorted = ctx.enter_context(nc.semaphore("pixels_sorted"))
        front_done = ctx.enter_context(nc.semaphore("front_done"))
        front_taken = ctx.enter_context(nc.semaphore("front_taken"))
        stats_ready = ctx.enter_context(nc.semaphore("stats_ready"))
        rstd_ready = ctx.enter_context(nc.semaphore("rstd_ready"))
        norm_ready = ctx.enter_context(nc.semaphore("norm_ready"))
        h_summed = ctx.enter_context(nc.semaphore("h_summed"))
        xn_ready = ctx.enter_context(nc.semaphore("xn_ready"))
        conv_ready = ctx.enter_context(nc.semaphore("conv_ready"))
        u_ready = ctx.enter_context(nc.semaphore("u_ready"))
        pre_ready = ctx.enter_context(nc.semaphore("pre_ready"))
        soft_ready = ctx.enter_context(nc.semaphore("soft_ready"))
        delta_ready = ctx.enter_context(nc.semaphore("delta_ready"))
        du_ready = ctx.enter_context(nc.semaphore("du_ready"))
        decay_log_ready = ctx.enter_context(nc.semaphore("decay_log_ready"))
        decays_ready = ctx.enter_context(nc.semaphore("decays_ready"))
        bc_ready = ctx.enter_context(nc.semaphore("bc_ready"))
        log15_ready = ctx.enter_context(nc.semaphore("log15_ready"))
        decays15_ready = ctx.enter_context(nc.semaphore("decays15_ready"))
        gated_ready = ctx.enter_context(nc.semaphore("gated_ready"))
        end_ready = ctx.enter_context(nc.semaphore("end_ready"))
        alive_ready = ctx.enter_context(nc.semaphore("alive_ready"))
        hot_ready = ctx.enter_context(nc.semaphore("hot_ready"))
        exp_ready = ctx.enter_context(nc.semaphore("exp_ready"))
        logits_ready = ctx.enter_context(nc.semaphore("logits_ready"))
        parts1_ready = ctx.enter_context(nc.semaphore("parts1_ready"))
        rest_ready = ctx.enter_context(nc.semaphore("rest_ready"))
        parts2_ready = ctx.enter_context(nc.semaphore("parts2_ready"))
        split_ready = ctx.enter_context(nc.semaphore("split_ready"))
        selfprod_ready = ctx.enter_context(nc.semaphore("selfprod_ready"))
        shift_ready = ctx.enter_context(nc.semaphore("shift_ready"))
        ones_ready = ctx.enter_context(nc.semaphore("ones_ready"))
        parts_out = ctx.enter_context(nc.semaphore("parts_out"))
        stack_in = ctx.enter_context(nc.semaphore("stack_in"))
        shift_out = ctx.enter_context(nc.semaphore("shift_out"))
        shift_in = ctx.enter_context(nc.semaphore("shift_in"))
        pv_done = ctx.enter_context(nc.semaphore("pv_done"))
        pv_taken = ctx.enter_context(nc.semaphore("pv_taken"))
        self_exp = ctx.enter_context(nc.semaphore("self_exp"))
        ao_ready = ctx.enter_context(nc.semaphore("ao_ready"))
        tree_ready = ctx.enter_context(nc.semaphore("tree_ready"))
        tree_gelu = ctx.enter_context(nc.semaphore("tree_gelu"))
        coef_ready = ctx.enter_context(nc.semaphore("coef_ready"))
        out_stored = ctx.enter_context(nc.semaphore("out_stored"))
        tail_flag = ctx.enter_context(nc.semaphore("tail_flag"))
        tail_bc = ctx.enter_context(nc.semaphore("tail_bc"))
        tail_log = ctx.enter_context(nc.semaphore("tail_log"))
        tail_exp = ctx.enter_context(nc.semaphore("tail_exp"))
        tail_used = ctx.enter_context(nc.semaphore("tail_used"))
        tail_chain = ctx.enter_context(nc.semaphore("tail_chain"))
        full = [ctx.enter_context(nc.semaphore(f"psum_full{k}")) for k in range(SLOTS)]
        free = [ctx.enter_context(nc.semaphore(f"psum_free{k}")) for k in range(SLOTS)]
        s_w = ctx.enter_context(nc.semaphore("weights_in"))
        s_setup_v = ctx.enter_context(nc.semaphore("setup_vector"))
        s_setup_g = ctx.enter_context(nc.semaphore("setup_gpsimd"))
        s_setup_a = ctx.enter_context(nc.semaphore("setup_scalar"))
        s_setup_t = ctx.enter_context(nc.semaphore("setup_tensor"))

        PS = ctx.enter_context(nc.psum_tensor("PS", [128, 8, 512], F32))
        ACC = PS[:, 6:8, :]

        def slot(name):
            return PS[:, 2 * SLOT[name]:2 * SLOT[name] + 2, :]

        def wide(name, n=128):
            return slot(name)[0:n, :, 0:CW]

        ident = sb("ident", [128, 128])
        identb = sb("identb", [128, 128], BF16)
        negbig = sb("negbig", [128, 128], BF16)
        ones = sb("ones", [128, 128])
        onesb = sb("onesb", [128, T2], BF16)
        first15 = sb("first15", [128, ND * NG * LS], BF16)
        clamp = sb("clamp", [128, 1])
        minus_half = sb("minus_half", [128, NT])
        rank8 = sb("rank8", [128, NT, E])
        w_tok1 = sb("w_tok1", [128, 4, D])
        w_tok2 = sb("w_tok2", [128, 2, D])
        base = sb("base", [128, NT, D])
        w_in = sb("w_in", [KD, 2, 2 * DI])
        w_norm = sb("w_norm", [KD, 2])
        conv_w = sb("conv_w", [128, ND, 4])
        conv_b = sb("conv_b", [128, ND])
        w_x = sb("w_x", [128, ND, KD])
        w_dt = sb("w_dt", [KD, DI])
        b_dt = sb("b_dt", [128, ND])
        Aneg = sb("Aneg", [128, ND, NS])
        Dp = sb("Dp", [128, ND])
        w_out = sb("w_out", [128, ND, D])
        sel_b = sb("sel_b", [KD, 2, 128])
        w_route = sb("w_route", [KD, 2, E])
        b_route = sb("b_route", [128, E])
        w_1 = sb("w_1", [KD, 2, E * R])
        b_1 = sb("b_1", [128, 4])
        w_2 = sb("w_2", [128, 4, D])
        b_2 = sb("b_2", [KD, 3, D], BF16)
        sel_e = sb("sel_e", [KD, 4, 128], BF16)
        w_qkv = sb("w_qkv", [KD, 2, 3 * D])
        self_w = sb("self_w", [KD, 2, H])
        w_pr = sb("w_pr", [KD, 2, D])
        b_pr = sb("b_pr", [128, D])
        w_tree = sb("w_tree", [KD, 2, NODES])
        w_leaf = sb("w_leaf", [KD, D])

        xin = sb("xin", [NY, C * 8, IMG])
        bl1 = sb("bl1", [128, NY, NY])
        bl2 = sb("bl2", [128, NY, NY])
        h = sb("h", [128, NT, D])
        xt = sb("xt", [128, NT, D])
        xT = sb("xT", [KD, 2, TW])
        st = sb("st", [128, NT, 6])
        mv = sb("mv", [128, NT, 2])
        rs = sb("rs", [128, 4, NT])
        prT = sb("prT", [KD, TW])
        gated = sb("gated", [128, 4, TW])
        tokT = gated[0:KD, 0:2, :]
        arena = sb("arena", [128, 14640])
        def rows(k):
            return arena[:, k * ND * TW:(k + 1) * ND * TW].rearrange("p (m t) -> p m t", m=ND)
        u, zs, dl, du, gg, lw = (rows(k) for k in range(6))
        xi = gg
        PT = arena[:, 0:8 * T2].rearrange("p (b t) -> p b t", b=8)
        Qs = arena[:, 8 * T2:14 * T2].bitcast(BF16).rearrange("p (h t) -> p h t", h=H)
        Ks = arena[:, 14 * T2:20 * T2].bitcast(BF16).rearrange("p (h t) -> p h t", h=H)
        qkf = sb("qkf", [128, 4, T2])
        xn = qkf[:, 0:2, :].rearrange("p a t -> p (a t)")[:, 0:NT * D].rearrange("p (j d) -> p j d", j=NT)
        OT = qkf[:, :, :].rearrange("p a t -> p (a t)")[:, 0:3 * TW].rearrange("p (g t) -> p g t", g=3)
        parts_f = sb("parts_f", [128, 6 * T2])
        parts = parts_f[0:KD, :].bitcast(BF16).rearrange("p (w i m t) -> p w i m t", w=2, i=3, m=2)
        def small(k):
            return parts_f[:, k * ND * NG * LS:(k + 1) * ND * NG * LS]
        g15, l15, x15, s15 = (small(k) for k in range(4))
        bdB = xT[:, 0, 0:NG * LS]
        bdC = xT[:, 1, 0:NG * LS]
        rest = PT
        prod = PT
        ends15 = sb("ends15", [128, 2, ND, NG])
        alive = sb("alive", [128, 2])
        flag = sb("flag", [128, 1], I32)
        logit = sb("logit", [128, NT, E])
        hot = sb("hot", [128, NT, E])
        best = sb("best", [128, 4, NT])
        hotT = sb("hotT", [KD, TW], BF16)
        V = sb("V", [128, NT, H, 32])
        smax = sb("smax", [128, H, NT])
        smid = sb("smid", [128, NT, H])
        sself = sb("sself", [128, NT, H])
        shift = sb("shift", [128, 3, NT, H])
        shiftT = sb("shiftT", [H, 2, T2], BF16)
        den = sb("den", [128, 2, H])
        tl = sb("tl", [128, NT, NODES])
        tc = sb("tc", [128, NT, NODES])
        ta = sb("ta", [128, NT, NODES])
        te = sb("te", [128, NT, NODES])
        cf = sb("cf", [128, NT, NODES])
        tsum = sb("tsum", [128, NT])
        mb = sb("mb", [128, 2, NT, H], BF16)
        coefT = prT

        scr_qk = nc.dram_tensor("scr_qk", (2, 3, D, T2), BF16).ap()
        scr_shift = nc.dram_tensor("scr_shift", (2, H, T2), BF16).ap()

        wp = arena[0:KD, 3000:4024].rearrange("p (m k x) -> p m k x", m=2, k=4)
        wp2 = arena[0:KD, 4024:4536].rearrange("p (m k x) -> p m k x", m=2, k=4)
        px1 = parts_f[0:NY, 0:NY * 128].rearrange("y (x n) -> y x n", n=128)
        px2 = qkf[0:NY, :, :].rearrange("y a t -> y (a t)")[:, 0:NY * 64].rearrange("y (x n) -> y x n", n=64)
        n_w = [0]

        with nc.Block() as block:
            @block.sync
            def _(sp):
                def load(dst, src, slow=False):
                    sp.dma_start(dst, src, allow_slow_non_contiguous=slow).then_inc(s_w, 16)
                    n_w[0] += 16
                sp.wait_ge(s_setup_v, 1)
                load(arena[0:KD, 0:1536].rearrange("p (m k) -> p m k", m=2),
                     ap["L0_tok_w"].rearrange("(m p) k -> p m k", p=KD))
                load(arena[0:KD, 1536:1664].rearrange("p (m r) -> p m r", m=2),
                     ap["L0_ffn_enc_w"].rearrange("(m p) r -> p m r", p=KD))
                load(arena[0:R, 1664:1672], ap["L0_ffn_sw_w"])
                load(arena[0:R, 1672:1673], ap["L0_ffn_enc_b"].rearrange("(r o) -> r o", o=1), slow=True)
                load(arena[0:NODES, 1680:1872], ap["L1_ffn_weights_in"])
                load(arena[0:E, 1872:2064], ap["L0_ffn_b2"])
                load(arena[:, 2064:2072], ap["L0_ffn_sw_b"].partition_broadcast(128))
                load(arena[0:KD, 2072:2084], ap["L1_attn_temperature"].rearrange("h a b -> (h a b)").partition_broadcast(KD))
                load(w_in[:, :, :], ap["L0_attn_w_in"].rearrange("(m p) n -> p m n", p=KD))
                load(w_norm[:, :], ap["L0_attn_w_norm"].rearrange("(m p) -> p m", p=KD), slow=True)
                load(conv_w[:, :, :], ap["L0_attn_conv_w"].rearrange("(m p) k -> p m k", p=128))
                load(conv_b[:, :], ap["L0_attn_conv_b"].rearrange("(m p) -> p m", p=128), slow=True)
                wx = ap["L0_attn_w_xproj"].rearrange("(m p) n -> p m n", p=128)
                load(w_x[:, :, 0:RANK], wx[:, :, 0:RANK])
                load(w_x[:, :, BROW:BROW + NS], wx[:, :, RANK:RANK + NS])
                load(w_x[:, :, CROW:CROW + NS], wx[:, :, RANK + NS:])
                load(w_dt[0:RANK, :], ap["L0_attn_w_dt"])
                load(b_dt[:, :], ap["L0_attn_b_dt"].rearrange("(m p) -> p m", p=128), slow=True)
                load(Aneg[:, :, :], ap["L0_attn_A_log"].rearrange("(m p) n -> p m n", p=128))
                load(Dp[:, :], ap["L0_attn_D_param"].rearrange("(m p) -> p m", p=128), slow=True)
                load(w_out[:, :, :], ap["L0_attn_w_out"].rearrange("(m p) n -> p m n", p=128))
                for k in range(2):
                    load(w_1[:, k, :].rearrange("p (e r) -> p e r", e=E),
                         ap["L0_ffn_w1"].rearrange("e (k p) r -> p k e r", p=KD)[:, k])
                load(b_1[:, :], ap["L0_ffn_b1"].rearrange("e r -> (e r)").rearrange("(m p) -> p m", p=128), slow=True)
                load(w_2[:, :, :], ap["L0_ffn_w2"].rearrange("e r n -> (e r) n").rearrange("(m p) n -> p m n", p=128))
                load(w_qkv[:, :, :], ap["L1_attn_w_qkv"].rearrange("(m p) n -> p m n", p=KD))
                load(w_pr[:, :, :], ap["L1_attn_w_proj"].rearrange("(m p) n -> p m n", p=KD))
                load(b_pr[:, :], ap["L1_attn_b_proj"].partition_broadcast(128))
                load(w_leaf[1:NODES, :], ap["L1_ffn_weights_out"][1:NODES, :])
                pos = ap["L0_tok_pos_embedding"][0]
                load(base[0:1, 0, :], ap["cls_tok"][0])
                load(base[1:128, 0, :], pos[0:127, :])
                load(base[:, 1:NT - 1, :], pos[127:127 + 128 * (NT - 2), :].rearrange("(j p) d -> p j d", p=128))
                load(base[0:LAST, NT - 1, :], pos[127 + 128 * (NT - 2):T - 1, :])
                for j in range(1, NT):
                    load(xt[:, j, :], ap["L0_tok_b"].partition_broadcast(128))
                load(xt[2:128, 0, :], ap["L0_tok_b"].partition_broadcast(126))
                load(xt[1:2, 0, :], ap["L0_tok_cls_token"][0])

            @block.gpsimd
            def _(g):
                g.sem_inc(out_stored, AHEAD["out_stored"])
                for k in range(SLOTS):
                    g.sem_inc(free[k], PSUM_AHEAD)
                g.memset(ident[:, :], 0.0).then_inc(s_setup_g, 1)
                g.wait_ge(s_setup_g, 1)
                g.affine_select(out=ident[:, :], in_=ident[:, :], compare_op=ALU.not_equal, fill=1.0,
                                base=0, pattern=[[-1, 128]], channel_multiplier=1).then_inc(s_setup_g, 1)
                g.wait_ge(s_setup_a, 1)
                v = self_w[:, :, :]
                g.affine_select(out=v, in_=v, compare_op=ALU.is_ge, fill=0.0, base=0,
                                pattern=[[KD, 2], [-DH, H]], channel_multiplier=1).then_inc(s_setup_g, 1)
                g.wait_ge(s_setup_g, 3)
                g.affine_select(out=v, in_=v, compare_op=ALU.is_ge, fill=0.0, base=DH - 1,
                                pattern=[[-KD, 2], [DH, H]], channel_multiplier=-1).then_inc(s_setup_g, 1)

            @block.vector
            def _(v):
                v.memset(arena[:, :], 0.0)
                v.memset(parts_f[:, :], 0.0)
                v.memset(qkf[:, :, :], 0.0)
                v.memset(xt[:, :, :], 0.0)
                v.memset(base[:, :, :], 0.0)
                v.memset(w_x[:, :, :], 0.0)
                v.memset(w_dt[:, :], 0.0)
                v.memset(ta[:, :, :], 1.0)
                v.memset(smid[:, :, :], 0.0)
                v.memset(w_leaf[:, :], 0.0).then_inc(s_setup_v, 1)
                for t, x in ((PS, 0.0), (ones, 1.0), (onesb, 1.0), (first15, 1.0), (clamp, CLAMP), (minus_half, -0.5),
                             (prT, 0.0), (gated, 0.0), (xT, 0.0), (hotT, 0.0), (V, 0.0), 
                             (b_2, 0.0), (xin, 0.0), (shiftT, 0.0), (h, 0.0), (st, 0.0), (mv, 0.0), (smax, 0.0)):
                    v.memset(t[tuple(slice(None) for _ in t.shape)], x).then_inc(s_setup_v, 1)
                for e in range(E):
                    v.memset(rank8[:, :, e], float(E - e)).then_inc(s_setup_v, 1)
                n = 1 + 18 + E
                v.wait_ge(s_setup_v, n)
                v.memset(first15[:, :].rearrange("p (a t) -> p a t", t=LS)[:, :, 0], 0.0)
                v.memset(V[:, :, :, DH:DH + 1], 1.0)
                v.wait_ge(s_w, n_w[0])
                for m in range(2):
                    v.tensor_scalar(w_in[:, m, :], w_in[:, m, :], w_norm[:, m:m + 1], None, ALU.mult)
                v.tensor_tensor(base[:, :, :], base[:, :, :], xt[:, :, :], ALU.add)
                for m in range(2):
                    src = arena[0:KD, 768 * m:768 * m + 768].rearrange("p (c a r e s) -> p a e c r s", c=C, a=2, r=8, e=2)
                    for a in range(2):
                        for e in range(2):
                            k = 2 * a + e
                            v.tensor_copy(wp[:, m, k, 0:128].rearrange("p (c r s) -> p c r s", c=2, r=8), src[:, a, e, 0:2])
                            ins = v.tensor_copy(wp2[:, m, k, :].rearrange("p (r s) -> p r s", r=8), src[:, a, e, 2])
                ins.then_inc(s_setup_v, 1)
                v.wait_ge(s_setup_v, n + 1)
                v.wait_ge(s_setup_g, 2)
                v.tensor_copy(identb[:, :], ident[:, :])
                v.tensor_scalar(negbig[:, :], ident[:, :], -BIG, None, ALU.mult)
                for k, row in enumerate((BROW, CROW)):
                    v.tensor_copy(sel_b[:, k, :], ident[0:KD, row:row + 1].to_broadcast([KD, 128]))
                for m in range(4):
                    for e in range(2):
                        v.tensor_copy(sel_e[:, m, R * e:R * e + R],
                                      ident[0:KD, 2 * m + e:2 * m + e + 1].to_broadcast([KD, R]))
                b2 = arena[0:E, 1872:2064]
                b2b = arena[0:E, 2100:2292]
                b2c = arena[0:E, 2292:2484]
                v.tensor_copy(b_2[0:E, 0, :], b2).then_inc(s_setup_v, 1)
                v.wait_ge(s_setup_v, n + 2)
                v.tensor_tensor(b2b, b2, b_2[0:E, 0, :], ALU.subtract).then_inc(s_setup_v, 1)
                v.wait_ge(s_setup_v, n + 3)
                v.tensor_copy(b_2[0:E, 1, :], b2b).then_inc(s_setup_v, 1)
                v.wait_ge(s_setup_v, n + 4)
                v.tensor_tensor(b2c, b2b, b_2[0:E, 1, :], ALU.subtract).then_inc(s_setup_v, 1)
                v.wait_ge(s_setup_v, n + 5)
                v.tensor_copy(b_2[0:E, 2, :], b2c).then_inc(s_setup_v, 1)
                v.wait_ge(s_setup_v, n + 6)
                v.wait_ge(s_setup_t, 1)
                v.tensor_copy(w_tok1[:, :, :].rearrange("p (b t) d -> p b (t d)", b=2), PS[:, 0:2, 0:2 * D])
                v.tensor_copy(w_tok2[:, :, :].rearrange("p t d -> p (t d)"), PS[:, 2, 0:2 * D])
                v.tensor_copy(arena[0:R, 2500:2500 + D], PS[0:R, 3, 0:D])
                v.tensor_copy(w_tree[:, :, :].rearrange("p m n -> p (m n)"), PS[0:KD, 4, 0:2 * NODES])
                v.tensor_copy(arena[0:R, 2700:2828], arena[0:R, 1672:1673].to_broadcast([R, 128])).then_inc(s_setup_v, 1)
                v.wait_ge(s_setup_t, 2)
                v.tensor_copy(w_route[:, :, :].rearrange("p m n -> p (m n)"), PS[0:KD, 5, 0:2 * E])
                v.tensor_tensor(b_route[:, :], arena[:, 2064:2072], PS[:, 6, 0:E], ALU.add)
                v.wait_ge(s_setup_a, 2)
                v.tensor_scalar(Aneg[:, :, :], Aneg[:, :, :], -1.0, None, ALU.mult).then_inc(s_setup_v, 1)

            @block.scalar
            def _(a):
                a.wait_ge(s_w, n_w[0])
                t_bc = arena[0:KD, 2072:2084]
                for m in range(2):
                    last = a.activation(self_w[:, m, :], t_bc, ACT.Copy, bias=0.25, scale=-0.25)
                last.then_inc(s_setup_a, 1)
                a.activation(Aneg[:, :, :], Aneg[:, :, :], ACT.Exp).then_inc(s_setup_a, 1)

            @block.tensor
            def _(t):
                t.wait_ge(s_w, n_w[0])
                t.wait_ge(s_setup_g, 2)
                t.wait_ge(s_setup_v, 1 + 18 + E + 1)
                for m in range(2):
                    for a in range(2):
                        for e in range(2):
                            t.transpose(PS[:, a, e * D + m * KD:e * D + (m + 1) * KD], wp[:, m, 2 * a + e, :],
                                        ident[0:KD, 0:KD])
                        t.transpose(PS[:, 2, a * D + m * KD:a * D + (m + 1) * KD],
                                    wp2[:, m, 2 * a:2 * a + 2, :].rearrange("p e x -> p (e x)"), ident[0:KD, 0:KD])
                    t.transpose(PS[0:R, 3, m * KD:(m + 1) * KD], arena[0:KD, 1536 + m * R:1536 + (m + 1) * R],
                                ident[0:KD, 0:KD])
                    last = t.transpose(PS[0:KD, 4, m * NODES:(m + 1) * NODES],
                                       arena[0:NODES, 1680 + m * KD:1680 + (m + 1) * KD], ident[0:NODES, 0:NODES])
                last.then_inc(s_setup_t, 1)
                t.wait_ge(s_setup_v, 1 + 18 + E + 1 + 5 + 1)
                for m in range(2):
                    t.matmul(PS[0:KD, 5, m * E:(m + 1) * E], lhsT=arena[0:R, 2500 + m * KD:2500 + (m + 1) * KD],
                             rhs=arena[0:R, 1664:1672], start=True, stop=True)
                t.matmul(PS[:, 6, 0:E], lhsT=arena[0:R, 2700:2828], rhs=arena[0:R, 1664:1672],
                         start=True, stop=True).then_inc(s_setup_t, 1)

        waits_apart = ctx.enter_context(nc.semaphore("waits_apart"))
        block = ctx.enter_context(nc.Block())

        def flat(job):
            return slot(job).rearrange("p b n -> p (b n)")

        def width(j):
            return LAST if j == NT - 1 else 128

        PARTS_Q = (0, 0, 1, 1, 0, 2)
        PARTS_K = (0, 1, 0, 1, 2, 0)

        @block.sync
        def _(sp):
            sp.dma_start(xin[:, :, :].rearrange("y (c r) w -> y c r w", c=C),
                         ap["x"][0].rearrange("c (y r) w -> y c r w", r=8)).then_inc(pixels_in, 16)
            with sp.Fori(0, B) as i:
                sp.wait_ge(pixels_sorted, at(i, "pixels_sorted", 0))
                sp.dma_start(xin[:, :, :].rearrange("y (c r) w -> y c r w", c=C),
                             ap["x"][(i + 1) % B].rearrange("c (y r) w -> y c r w", r=8)).then_inc(pixels_in, 16)
                for w in range(2):
                    sp.wait_ge(split_ready, at(i, "split_ready", 2 * w + 2))
                    for n in range(2):
                        sp.dma_start(scr_qk[w].rearrange("t (m p) c -> p t m c", p=KD)[:, :, n], parts[:, w, :, n]) \
                            .then_inc(parts_out, 16)
                sp.wait_ge(parts_out, at(i, "parts_out", 64))
                for w, (dst, order) in enumerate(((Qs, PARTS_Q), (Ks, PARTS_K))):
                    for n, part in enumerate(order):
                        sp.dma_start(dst[DH * n:DH * n + DH, :, :],
                                     scr_qk[w, part].rearrange("(h d) c -> d h c", d=DH)).then_inc(stack_in, 16)
                for n in range(2):
                    sp.wait_ge(free[SLOT[f"shiftT{n}"]], freed(i, f"shiftT{n}"))
                    sp.dma_start(scr_shift[n], shiftT[:, n, :]).then_inc(shift_out, 16)
                sp.wait_ge(shift_out, at(i, "shift_out", 32))
                for n in range(2):
                    sp.dma_start(Qs[KD + n:KD + n + 1, :, :], scr_shift[n:n + 1]).then_inc(shift_in, 16)
                sp.wait_ge(free[SLOT["out1"]], freed(i, "out1"))
                sp.dma_start(out[i, 0:128 * (NT - 1), :].rearrange("(j p) d -> p j d", p=128),
                             xt[:, 0:NT - 1, :]).then_inc(out_stored, 16)
                sp.dma_start(out[i, 128 * (NT - 1):T, :], xt[0:LAST, NT - 1, :]).then_inc(out_stored, 16)
            sp.wait_ge(out_stored, B * COUNTS["out_stored"] + AHEAD["out_stored"])

        @block.gpsimd
        def _(g):
            by_block = xin[:, :, :].rearrange("y r (x s) -> y r x s", s=8)

            def sort(px, r0, r1):
                for r in range(r0, r1, 8):
                    ins = g.tensor_scalar(px[:, :, 8 * (r - r0):8 * (r - r0) + 64].rearrange("y x (r s) -> y r x s", s=8),
                                          by_block[:, r:r + 8], 1.0, 0.0, ALU.mult, ALU.add)
                return ins

            g.wait_ge(pixels_in, 16)
            g.sem_inc(waits_apart, 1)
            sort(px2, 16, 24).then_inc(pixels_sorted, 1)
            sort(px1, 0, 16).then_inc(pixels_sorted, 1)
            with g.Fori(0, B) as i:
                links = [0]

                def link(ins):
                    links[0] += 1
                    ins.then_inc(pool_chain, 1)
                    g.wait_ge(pool_chain, at(i, "pool_chain", links[0]))

                for k in range(4):
                    g.wait_ge(stats_ready, at(i, "stats_ready", k + 1))
                    g.sem_inc(waits_apart, 1)
                    link(g.tensor_scalar(rs[:, 2, :], mv[:, :, 1], EPS, None, ALU.add))
                    pw = g.tensor_tensor(rs[:, 0, :], rs[:, 2, :], minus_half[:, :], ALU.pow)
                    if k == 0:
                        link(pw)
                        link(g.tensor_tensor(rs[:, 3, :], mv[:, :, 1], rs[:, 0, :], ALU.mult))
                        link(g.tensor_tensor(rs[:, 3, :], rs[:, 3, :], rs[:, 0, :], ALU.mult))
                        g.sem_inc(waits_apart, 1)
                        link(g.tensor_scalar(rs[:, 3, :], rs[:, 3, :], EPS, None, ALU.add))
                        pw = g.tensor_tensor(rs[:, 1, :], rs[:, 3, :], minus_half[:, :], ALU.pow)
                    pw.then_inc(rstd_ready, 1)
                    g.wait_ge(rstd_ready, at(i, "rstd_ready", k + 1))
                    if k == 0:
                        g.wait_ge(norm_ready, at(i, "norm_ready", 1))
                        g.tensor_tensor(h[:, :, :], h[:, :, :], xt[:, :, :], ALU.add).then_inc(h_summed, 1)
                        for m in range(ND):
                            g.wait_ge(delta_ready, at(i, "delta_ready", m + 1))
                            g.tensor_tensor(du[:, m, 0:T2], dl[:, m, 0:T2], u[:, m, 0:T2], ALU.mult).then_inc(du_ready, 1)
                        g.wait_ge(end_ready, at(i, "end_ready", 1))
                        g.sem_inc(waits_apart, 1)
                        g.partition_all_reduce(alive[:, 1:2], alive[:, 0:1], 128, bass.bass_isa.ReduceOp.max).then_inc(alive_ready, 1)
                    if k == 2:
                        g.wait_ge(norm_ready, at(i, "norm_ready", 3))
                        g.tensor_tensor(h[:, :, :], h[:, :, :],
                                        b_pr[:, :].unsqueeze(1).to_broadcast([128, NT, D]), ALU.add).then_inc(h_summed, 1)
                        g.wait_ge(h_summed, at(i, "h_summed", 2))
                        g.sem_inc(waits_apart, 1)
                        g.memset(Ks[KD:KD + 2, :, :], 1.0).then_inc(ones_ready, 1)
                        g.wait_ge(pixels_in, at(i, "pixels_in", 16))
                        g.wait_ge(selfprod_ready, at(i, "selfprod_ready", 2))
                        g.sem_inc(waits_apart, 1)
                        sort(px2, 16, 24).then_inc(pixels_sorted, 1)
                        g.wait_ge(parts_out, at(i, "parts_out", 64))
                        g.sem_inc(waits_apart, 1)
                        sort(px1, 0, 16).then_inc(pixels_sorted, 1)
                assert links[0] == COUNTS["pool_chain"], links

        @block.scalar
        def _(a):
            def take_blocks(n):
                dst, nx = (bl2, 14 - n % 2) if n < 2 else (bl1, 14)
                x0 = 14 * (n % 2)
                return a.activation(dst[:, :, x0:x0 + nx].rearrange("p y x -> p x y"),
                                    ACC[:, n % 2, 0:nx * NY].rearrange("p (x y) -> p x y", y=NY), ACT.Copy)

            def take_patches(n):
                m, c = divmod(n, 2)
                rows_y = 14 - c
                return a.activation(tokT[:, m, 2 + 14 * OUT * c:2 + 14 * OUT * c + rows_y * OUT],
                                    ACC[0:KD, c, 0:rows_y * OUT], ACT.Copy)

            for n in range(4):
                a.wait_ge(front_done, n + 1)
                take_blocks(n).then_inc(front_taken, 1)
            for n in range(4):
                a.wait_ge(front_done, n + 5)
                take_patches(n).then_inc(front_taken, 1)
            with a.Fori(0, B) as i:
                links = [0]

                def link(ins):
                    links[0] += 1
                    ins.then_inc(act_chain, 1)
                    a.wait_ge(act_chain, at(i, "act_chain", links[0]))

                def transposed(name):
                    for m in range(2):
                        a.wait_ge(full[SLOT[f"{name}{m}"]], filled(i, f"{name}{m}"))
                        a.activation(xT[:, m, :], flat(f"{name}{m}")[0:KD, 0:TW], ACT.Copy).then_inc(free[SLOT[f"{name}{m}"]], 1)

                a.wait_ge(norm_ready, at(i, "norm_ready", 1))
                a.wait_ge(rstd_ready, at(i, "rstd_ready", 1))
                for j in range(NT):
                    ins = a.activation(xn[:, j, :], xt[:, j, :], ACT.Copy, scale=rs[:, 1, j:j + 1])
                ins.then_inc(xn_ready, 1)
                transposed("xnT")
                for m in range(ND):
                    a.wait_ge(full[SLOT[f"xz{m}"]], filled(i, f"xz{m}"))
                    ins = a.activation(xi[:, m, 3:3 + T2].rearrange("p (b t) -> p b t", b=2), wide(f"xz{m}"), ACT.Copy)
                    ins.then_inc(free[SLOT[f"xz{m}"]], 1)
                for m in range(ND):
                    a.wait_ge(full[SLOT[f"xz{ND + m}"]], filled(i, f"xz{ND + m}"))
                    ins = a.activation(zs[:, m, 0:T2].rearrange("p (b t) -> p b t", b=2), wide(f"xz{ND + m}"), ACT.Silu)
                    ins.then_inc(free[SLOT[f"xz{ND + m}"]], 1)
                for m in range(ND):
                    a.wait_ge(conv_ready, at(i, "conv_ready", m + 1))
                    a.activation(u[:, m, 0:T2], gated[:, m, 0:T2], ACT.Silu).then_inc(u_ready, 1)
                a.wait_ge(full[SLOT["proj"]], filled(i, "proj"))
                a.activation(prT[:, 0:T2].rearrange("p (b t) -> p b t", b=2), wide("proj", KD), ACT.Copy).then_inc(free[SLOT["proj"]], 1)
                for m in range(ND):
                    a.wait_ge(pre_ready, at(i, "pre_ready", m + 1))
                    link(a.activation(dl[:, m, 0:T2], dl[:, m, 0:T2], ACT.Exp))
                    a.activation(dl[:, m, 0:T2], dl[:, m, 0:T2], ACT.Ln, bias=1.0).then_inc(soft_ready, 1)
                for m in range(ND):
                    a.wait_ge(decay_log_ready, at(i, "decay_log_ready", m + 1))
                    a.activation(gg[:, m, 0:T2], gg[:, m, 0:T2], ACT.Exp)
                    a.activation(lw[:, m, 0:T2], lw[:, m, 0:T2], ACT.Exp, bias=clamp[:, :]).then_inc(decays_ready, 1)
                a.wait_ge(log15_ready, at(i, "log15_ready", 1))
                a.activation(g15, g15, ACT.Exp)
                a.activation(s15, l15, ACT.Exp, bias=clamp[:, :]).then_inc(decays15_ready, 1)
                a.wait_ge(tail_flag, at(i, "tail_flag", 1))
                a.sem_inc(waits_apart, 1)
                with a.If(a.value_load(flag[0:1, 0:1]) != 0):
                    with a.Fori(0, NG) as n:
                        for m in range(ND):
                            a.wait_ge(tail_log, i * COUNTS["tail_log"] + n * ND + (m + 1))
                            a.activation(gg[:, m, LS:T2], gg[:, m, LS:T2], ACT.Exp)
                            a.activation(lw[:, m, LS:T2], lw[:, m, LS:T2], ACT.Exp, bias=clamp[:, :]) \
                                .then_inc(tail_exp, 1)
                with a.Else():
                    a.sem_inc(tail_exp, COUNTS["tail_exp"])

                transposed("x2T")
                a.wait_ge(logits_ready, at(i, "logits_ready", 1))
                a.activation(logit[:, :, :], hot[:, :, :], ACT.Exp).then_inc(exp_ready, 1)
                a.wait_ge(full[SLOT["hotT"]], filled(i, "hotT"))
                a.activation(hotT[0:E, :], flat("hotT")[0:E, 0:TW], ACT.Copy).then_inc(free[SLOT["hotT"]], 1)
                for m in range(4):
                    a.wait_ge(full[SLOT[f"hid{m}"]], filled(i, f"hid{m}"))
                    ins = a.activation(gated[:, m, 0:T2].rearrange("p (b t) -> p b t", b=2), wide(f"hid{m}"), ACT.Gelu,
                                       bias=b_1[:, m:m + 1])
                    ins.then_inc(free[SLOT[f"hid{m}"]], 1)

                transposed("x3T")
                for n, job in enumerate(("q0", "q1", "k0", "k1")):
                    a.wait_ge(full[SLOT[job]], filled(i, job))
                    ins = a.activation(qkf[0:KD, n, :].rearrange("p (b t) -> p b t", b=2), wide(job, KD), ACT.Copy,
                                       scale=DH ** -0.5 if n < 2 else 1.0)
                    ins.then_inc(free[SLOT[job]], 1)
                    a.wait_ge(free[SLOT[job]], freed(i, job))
                    a.activation(parts[:, n // 2, 0, n % 2, :], qkf[0:KD, n, :], ACT.Copy).then_inc(parts1_ready, 1)
                for n in range(4):
                    a.wait_ge(rest_ready, at(i, "rest_ready", n + 1))
                    a.activation(parts[:, n // 2, 1, n % 2, :], rest[0:KD, n, :], ACT.Copy).then_inc(parts2_ready, 1)
                for q, (j0, nj) in enumerate(HALVES):
                    a.wait_ge(full[SLOT[f"v{q}"]], filled(i, f"v{q}"))
                    nb = nj // 2
                    a.activation(V[:, j0:j0 + nj, :, 0:DH].rearrange("p (b j) h d -> p b (j h) d", b=nb),
                                            slot(f"v{q}")[:, 0:nb, 0:2 * D].rearrange("p b (x d) -> p b x d", d=DH),
                                            ACT.Copy).then_inc(free[SLOT[f"v{q}"]], 1)
                for n in range(4):
                    a.wait_ge(front_done, at(i, "front_done", n + 1))
                    take_blocks(n).then_inc(front_taken, 1)
                a.activation(tokT[:, :, 0:2], ident[0:KD, 124:128].rearrange("p (m c) -> p m c", m=2), ACT.Copy)
                for n in range(4):
                    a.wait_ge(front_done, at(i, "front_done", n + 5))
                    take_patches(n).then_inc(front_taken, 1)
                for n in range(2):
                    a.wait_ge(full[SLOT[f"shiftT{n}"]], filled(i, f"shiftT{n}"))
                    ins = a.activation(shiftT[:, n, :], flat(f"shiftT{n}")[0:H, 0:T2], ACT.Copy)
                    ins.then_inc(free[SLOT[f"shiftT{n}"]], 1)
                a.wait_ge(shift_ready, at(i, "shift_ready", 1))
                a.activation(sself[:, :, :], smid[:, :, :], ACT.Exp).then_inc(self_exp, 1)
                for g in range(3):
                    for j in range(NT):
                        n = g * NT + j
                        if n >= 2:
                            a.wait_ge(pv_done, at(i, "pv_done", n - 1))
                        for hh in range(4):
                            job = f"ST{4 * g + hh}_{j}"
                            w = width(j)
                            a.wait_ge(full[SLOT[job]], filled(i, job))
                            ins = a.activation(PT[0:w, 4 * (n % 2) + hh, :].rearrange("p (b t) -> p b t", b=2),
                                               wide(job, w), ACT.Exp)
                            ins.then_inc(free[SLOT[job]], 1)
                for m in range(2):
                    a.wait_ge(full[SLOT[f"aoT{m}"]], filled(i, f"aoT{m}"))
                    a.activation(xT[:, m, :], flat(f"aoT{m}")[0:KD, 0:TW], ACT.Copy).then_inc(free[SLOT[f"aoT{m}"]], 1)

                transposed("x4T")
                a.wait_ge(tree_ready, at(i, "tree_ready", 1))
                a.activation(te[:, :, :], tl[:, :, :], ACT.Gelu).then_inc(tree_gelu, 1)
                a.wait_ge(full[SLOT["coefT"]], filled(i, "coefT"))
                a.activation(coefT[0:NODES, :], flat("coefT")[0:NODES, 0:TW], ACT.Copy).then_inc(free[SLOT["coefT"]], 1)
                assert links[0] == COUNTS["act_chain"], links

        @block.vector
        def _(v):
            with v.Fori(0, B) as i:
                links = [0]

                def link(ins):
                    links[0] += 1
                    ins.then_inc(dve_chain, 1)
                    v.wait_ge(dve_chain, at(i, "dve_chain", links[0]))


                def pairs(job, nj):
                    return slot(job)[:, 0:nj // 2, 0:2 * D]

                def tiles(x, j0, nj):
                    return x[:, j0:j0 + nj, :].rearrange("p (b j) d -> p b (j d)", j=2)

                def layernorm(k):
                    for j in range(NT):
                        ins = v.bn_stats(st[:, j, :], h[:, j, :])
                    link(ins)
                    v.sem_inc(waits_apart, 1)
                    for j in range(NT):
                        ins = v.bn_aggr(mv[:, j, :], st[:, j, :])
                    ins.then_inc(stats_ready, 1)
                    v.wait_ge(stats_ready, at(i, "stats_ready", k + 1))
                    v.wait_ge(rstd_ready, at(i, "rstd_ready", k + 1))
                    if k == 0:
                        v.wait_ge(out_stored, at(i, "out_stored", 0))
                        v.sem_inc(waits_apart, 1)
                    for j in range(NT):
                        ins = v.tensor_scalar(xt[:, j, :], h[:, j, :], mv[:, j, 0:1], rs[:, 0, j:j + 1],
                                              ALU.subtract, ALU.mult)
                    ins.then_inc(norm_ready, 1)
                    v.wait_ge(norm_ready, at(i, "norm_ready", k + 1))

                def add_to_h(name, src=h, dst=h):
                    for q, (j0, nj) in enumerate(HALVES):
                        v.wait_ge(full[SLOT[f"{name}{q}"]], filled(i, f"{name}{q}"))
                        ins = v.tensor_tensor(tiles(dst, j0, nj), pairs(f"{name}{q}", nj), tiles(src, j0, nj), ALU.add)
                        ins.then_inc(free[SLOT[f"{name}{q}"]], 1)
                    v.wait_ge(free[SLOT[f"{name}1"]], freed(i, f"{name}1"))

                add_to_h("emb", base)
                layernorm(0)

                v.wait_ge(free[SLOT["xz0"]], freed(i, "xz0"))
                link(v.memset(xi[:, :, 0:3], 0.0))
                for m in range(ND):
                    v.wait_ge(free[SLOT[f"xz{m}"]], freed(i, f"xz{m}"))
                    yc = gated[:, m, 0:T2]
                    link(v.tensor_scalar(yc, xi[:, m, 0:T2], conv_w[:, m, 0:1], conv_b[:, m:m + 1], ALU.mult, ALU.add))
                    for k in range(1, 4):
                        ins = v.scalar_tensor_tensor(yc, xi[:, m, k:k + T2], conv_w[:, m, k:k + 1], yc, ALU.mult, ALU.add)
                        if k < 3:
                            link(ins)
                    ins.then_inc(conv_ready, 1)

                def halves(x):
                    return x.rearrange("p (b t) -> p b t", b=2)
                for m in range(ND):
                    v.wait_ge(full[SLOT[f"dt{m}"]], filled(i, f"dt{m}"))
                    v.tensor_scalar(halves(dl[:, m, 0:T2]), wide(f"dt{m}"), b_dt[:, m:m + 1], 40.0,
                                              ALU.add, ALU.min).then_inc(pre_ready, 1)
                for m in range(ND):
                    v.wait_ge(soft_ready, at(i, "soft_ready", m + 1))
                    v.scalar_tensor_tensor(halves(dl[:, m, 0:T2]), wide(f"dt{m}"), b_dt[:, m:m + 1],
                                                      halves(dl[:, m, 0:T2]), ALU.add, ALU.max).then_inc(free[SLOT[f"dt{m}"]], 1)
                    v.wait_ge(free[SLOT[f"dt{m}"]], freed(i, f"dt{m}"))
                    v.tensor_scalar(gg[:, m, 0:T2], dl[:, m, 0:T2], Aneg[:, m, 0:1], LOW,
                                                   ALU.mult, ALU.max).then_inc(delta_ready, 1)
                    v.wait_ge(delta_ready, at(i, "delta_ready", m + 1))
                    v.tensor_tensor_scan(lw[:, m, 0:T2], onesb[:, :], gg[:, m, 0:T2], 0.0,
                                                   ALU.mult, ALU.add).then_inc(decay_log_ready, 1)
                v.wait_ge(free[SLOT["proj"]], freed(i, "proj"))
                for row, bd in ((BROW, bdB), (CROW, bdC)):
                    ins = v.tensor_tensor(bd.rearrange("p (n t) -> p n t", t=LS),
                                          prT[:, 0:LS].unsqueeze(1).to_broadcast([KD, NG, LS]),
                                          ident[0:KD, row + 1:row + NS].unsqueeze(2).to_broadcast([KD, NG, LS]), ALU.mult)
                ins.then_inc(bc_ready, 1)

                def by_state(x):
                    return x.rearrange("p (m n t) -> p m n t", m=ND, n=NG)
                for m in range(ND):
                    ins = v.tensor_tensor(by_state(g15)[:, m], dl[:, m, 0:LS].unsqueeze(1).to_broadcast([128, NG, LS]),
                                          Aneg[:, m, 1:NS].unsqueeze(2).to_broadcast([128, NG, LS]), ALU.mult)
                link(ins)
                link(v.tensor_scalar(g15, g15, LOW, None, ALU.max))
                v.tensor_tensor_scan(l15, first15[:, :], g15, 0.0, ALU.mult, ALU.add).then_inc(log15_ready, 1)

                v.wait_ge(full[SLOT["B0"]], filled(i, "B0"))
                v.wait_ge(full[SLOT["C0"]], filled(i, "C0"))
                for m in range(ND):
                    y = gated[:, m, 0:T2]
                    v.wait_ge(decays_ready, at(i, "decays_ready", m + 1))
                    v.wait_ge(du_ready, at(i, "du_ready", m + 1))
                    ins = v.tensor_tensor(halves(y), halves(du[:, m, 0:T2]), wide("B0"), ALU.mult)
                    if m == ND - 1:
                        ins.then_inc(free[SLOT["B0"]], 1)
                        v.wait_ge(free[SLOT["B0"]], freed(i, "B0"))
                    else:
                        link(ins)
                    link(v.scalar_tensor_tensor(lw[:, m, 0:T2], lw[:, m, 0:T2], 1.0, y, ALU.min, ALU.mult))
                    link(v.tensor_tensor_scan(gg[:, m, 0:T2], gg[:, m, 0:T2], lw[:, m, 0:T2], 0.0, ALU.mult, ALU.add))
                    ins = v.tensor_tensor(halves(y), halves(gg[:, m, 0:T2]), wide("C0"), ALU.mult)
                    if m == ND - 1:
                        ins.then_inc(free[SLOT["C0"]], 1)
                        v.wait_ge(free[SLOT["C0"]], freed(i, "C0"))
                    else:
                        link(ins)
                    link(v.scalar_tensor_tensor(y, u[:, m, 0:T2], Dp[:, m:m + 1], y, ALU.mult, ALU.add))

                v.wait_ge(full[SLOT["BC15"]], filled(i, "BC15"))
                v.wait_ge(decays15_ready, at(i, "decays15_ready", 1))
                v.memset(by_state(g15)[:, :, :, 0], 0.0)
                v.tensor_copy(ends15[:, 0], by_state(l15)[:, :, :, LS - 1])
                v.tensor_reduce(alive[:, 0:1], by_state(l15)[:, :, :, LS - 1], AX.XY, ALU.max).then_inc(end_ready, 1)
                B15 = slot("BC15")[:, 0, 0:NG * LS].rearrange("p (n t) -> p n t", t=LS)
                C15 = slot("BC15")[:, 1, 0:NG * LS].rearrange("p (n t) -> p n t", t=LS)
                for m in range(ND):
                    ins = v.tensor_tensor(by_state(x15)[:, m], du[:, m, 0:LS].unsqueeze(1).to_broadcast([128, NG, LS]),
                                          B15, ALU.mult)
                link(ins)
                link(v.scalar_tensor_tensor(x15, s15, 1.0, x15, ALU.min, ALU.mult))
                link(v.tensor_tensor_scan(s15, g15, x15, 0.0, ALU.mult, ALU.add))
                v.tensor_copy(ends15[:, 1], by_state(s15)[:, :, :, LS - 1])
                for m in range(ND):
                    ins = v.tensor_tensor(by_state(x15)[:, m], by_state(s15)[:, m], C15, ALU.mult)
                ins.then_inc(free[SLOT["BC15"]], 1)
                v.wait_ge(free[SLOT["BC15"]], freed(i, "BC15"))
                y15 = g15[:, 0:ND * LS].rearrange("p (m t) -> p m t", m=ND)
                for m in range(ND):
                    ins = v.tensor_reduce(y15[:, m], by_state(x15)[:, m].rearrange("p n t -> p t n"), AX.X, ALU.add)
                link(ins)
                link(v.tensor_tensor(gated[:, 0:ND, 0:LS], gated[:, 0:ND, 0:LS], y15, ALU.add))
                v.wait_ge(alive_ready, at(i, "alive_ready", 1))
                v.tensor_scalar(flag[0:1, :], alive[0:1, 1:2], DEAD, None, ALU.is_gt).then_inc(tail_flag, 1)
                v.wait_ge(tail_flag, at(i, "tail_flag", 1))
                v.sem_inc(waits_apart, 1)
                with v.If(v.value_load(flag[0:1, 0:1]) != 0):
                    with v.Fori(0, NG) as n:
                        steps = [0]

                        def tail_link(ins):
                            steps[0] += 1
                            ins.then_inc(tail_chain, 1)
                            v.wait_ge(tail_chain, i * COUNTS["tail_chain"] + n * TAIL_STEPS + steps[0])
                        for m in range(ND):
                            tail_link(v.tensor_scalar(gg[:, m, LS:T2], dl[:, m, LS:T2], Aneg[:, m, bass.ds(n + 1, 1)], LOW,
                                                      ALU.mult, ALU.max))
                            v.tensor_tensor_scan(lw[:, m, LS:T2], onesb[:, LS:T2], gg[:, m, LS:T2],
                                                 ends15[:, 0, m, bass.ds(n, 1)], ALU.mult, ALU.add).then_inc(tail_log, 1)
                        v.wait_ge(tail_bc, i * COUNTS["tail_bc"] + n + 1)
                        x = gated[:, ND, 0:T2]
                        for m in range(ND):
                            v.wait_ge(tail_exp, i * COUNTS["tail_exp"] + n * ND + (m + 1))
                            tail_link(v.tensor_tensor(halves(x), halves(du[:, m, 0:T2]), ACC[:, :, 0:CW], ALU.mult))
                            tail_link(v.scalar_tensor_tensor(lw[:, m, LS:T2], lw[:, m, LS:T2], 1.0, x[:, LS:T2],
                                                             ALU.min, ALU.mult))
                            tail_link(v.tensor_tensor_scan(gg[:, m, LS:T2], gg[:, m, LS:T2], lw[:, m, LS:T2],
                                                           ends15[:, 1, m, bass.ds(n, 1)], ALU.mult, ALU.add))
                            tail_link(v.tensor_tensor(halves(x), halves(gg[:, m, 0:T2]), PS[:, 0:2, 0:CW], ALU.mult))
                            ins = v.tensor_tensor(gated[:, m, LS:T2], gated[:, m, LS:T2], x[:, LS:T2], ALU.add)
                            if m < ND - 1:
                                tail_link(ins)
                            else:
                                ins.then_inc(tail_used, 1)
                                v.wait_ge(tail_used, i * COUNTS["tail_used"] + n + 1)
                        assert steps[0] == TAIL_STEPS, steps
                with v.Else():
                    v.sem_inc(tail_log, COUNTS["tail_log"])
                    v.sem_inc(tail_used, COUNTS["tail_used"])
                    v.sem_inc(tail_chain, COUNTS["tail_chain"])

                for m in range(ND):
                    ins = v.tensor_tensor(gated[:, m, 0:T2], gated[:, m, 0:T2], zs[:, m, 0:T2], ALU.mult)
                ins.then_inc(gated_ready, 1)
                v.wait_ge(h_summed, at(i, "h_summed", 1))
                add_to_h("mix")

                layernorm(1)
                v.wait_ge(full[SLOT["route"]], filled(i, "route"))
                ins = v.tensor_tensor(logit[:, :, :], slot("route")[:, 0, 0:NT * E].rearrange("p (j e) -> p j e", e=E),
                                      b_route[:, :].unsqueeze(1).to_broadcast([128, NT, E]), ALU.add)
                ins.then_inc(free[SLOT["route"]], 1)
                v.wait_ge(free[SLOT["route"]], freed(i, "route"))
                link(v.tensor_reduce(best[:, 0, :], logit[:, :, :], AX.X, ALU.max))
                v.tensor_tensor(hot[:, :, :], logit[:, :, :], best[:, 0, :].unsqueeze(2).to_broadcast([128, NT, E]),
                                          ALU.subtract).then_inc(logits_ready, 1)
                v.wait_ge(exp_ready, at(i, "exp_ready", 1))
                link(v.tensor_reduce(best[:, 1, :], logit[:, :, :], AX.X, ALU.add))
                link(v.reciprocal(best[:, 3, :], best[:, 1, :]))
                link(v.scalar_tensor_tensor(hot[:, :, :].rearrange("p j e -> p (j e)"),
                                               hot[:, :, :].rearrange("p j e -> p (j e)"), 0.0,
                                               rank8[:, :, :].rearrange("p j e -> p (j e)"), ALU.is_equal, ALU.mult))
                link(v.tensor_reduce(best[:, 2, :], hot[:, :, :], AX.X, ALU.max))
                v.tensor_tensor(hot[:, :, :], hot[:, :, :], best[:, 2, :].unsqueeze(2).to_broadcast([128, NT, E]),
                                          ALU.is_equal).then_inc(hot_ready, 1)
                for m in range(4):
                    v.wait_ge(full[SLOT[f"mask{m}"]], filled(i, f"mask{m}"))
                    v.wait_ge(free[SLOT[f"hid{m}"]], freed(i, f"hid{m}"))
                    v.tensor_tensor(halves(gated[:, m, 0:T2]), wide(f"mask{m}"), halves(gated[:, m, 0:T2]),
                                               ALU.mult).then_inc(free[SLOT[f"mask{m}"]], 1)
                for q, (j0, nj) in enumerate(HALVES):
                    v.wait_ge(full[SLOT[f"ffn{q}"]], filled(i, f"ffn{q}"))
                    for j in range(nj):
                        ins = v.scalar_tensor_tensor(h[:, j0 + j, :], slot(f"ffn{q}")[:, j // 2, D * (j % 2):D * (j % 2) + D],
                                                     best[:, 3, j0 + j:j0 + j + 1], h[:, j0 + j, :], ALU.mult, ALU.add)
                    ins.then_inc(free[SLOT[f"ffn{q}"]], 1)
                v.wait_ge(free[SLOT["ffn1"]], freed(i, "ffn1"))

                layernorm(2)
                for n in range(4):
                    v.wait_ge(parts1_ready, at(i, "parts1_ready", n + 1))
                    v.tensor_tensor(rest[0:KD, n, :], qkf[0:KD, n, :], parts[:, n // 2, 0, n % 2, :],
                                              ALU.subtract).then_inc(rest_ready, 1)
                for m in range(2):
                    v.tensor_tensor(prod[0:KD, 4 + m, :], qkf[0:KD, m, :], qkf[0:KD, 2 + m, :], ALU.mult).then_inc(selfprod_ready, 1)
                for n in range(4):
                    v.wait_ge(parts2_ready, at(i, "parts2_ready", n + 1))
                    v.tensor_tensor(parts[:, n // 2, 2, n % 2, :], rest[0:KD, n, :], parts[:, n // 2, 1, n % 2, :],
                                              ALU.subtract).then_inc(split_ready, 1)
                v.wait_ge(full[SLOT["self"]], filled(i, "self"))
                sv = slot("self")[:, 0, 0:NT * H].rearrange("p (j h) -> p j h", h=H)
                v.tensor_copy(smid[:, 0:NT - 1, :], sv[:, 0:NT - 1])
                v.tensor_copy(smid[0:LAST, NT - 1, :], sv[0:LAST, NT - 1]).then_inc(free[SLOT["self"]], 1)
                for hd in range(H):
                    for j in range(NT):
                        job = f"S{hd}_{j}"
                        w = width(j)
                        v.wait_ge(full[SLOT[job]], filled(i, job))
                        v.tensor_reduce(smax[0:w, hd, j:j + 1], wide(job, w), AX.XY, ALU.max).then_inc(free[SLOT[job]], 1)
                v.wait_ge(free[SLOT["S11_5"]], freed(i, "S11_5"))
                v.wait_ge(free[SLOT["self"]], freed(i, "self"))
                link(v.tensor_tensor(shift[:, 2], smax[:, :, :].rearrange("p h j -> p j h"), smid[:, :, :], ALU.max))
                link(v.tensor_scalar(shift[:, 2], shift[:, 2], -1.0, None, ALU.mult))
                link(v.tensor_copy(mb[:, 0], shift[:, 2]))
                link(v.tensor_copy(shift[:, 0], mb[:, 0]))
                link(v.tensor_tensor(shift[:, 2], shift[:, 2], shift[:, 0], ALU.subtract))
                link(v.tensor_copy(mb[:, 1], shift[:, 2]))
                link(v.tensor_copy(shift[:, 1], mb[:, 1]))
                link(v.tensor_tensor(shift[:, 2], shift[:, 0], shift[:, 1], ALU.add))
                v.tensor_tensor(smid[:, :, :], smid[:, :, :], shift[:, 2], ALU.add).then_inc(shift_ready, 1)
                for g in range(3):
                    v.wait_ge(pv_done, at(i, "pv_done", NT * (g + 1)))
                    v.tensor_copy(halves(OT[:, g, 0:T2]), ACC[:, :, 0:CW]).then_inc(pv_taken, 1)
                v.wait_ge(self_exp, at(i, "self_exp", 1))
                for q in range(3):
                    v.wait_ge(full[SLOT[f"oT{q}"]], filled(i, f"oT{q}"))
                    ov = slot(f"oT{q}")[:, :, 0:3 * 128].rearrange("p j (h d) -> p j h d", d=32)
                    spans = [(0, 2, 128)] if q < 2 else [(0, 1, 128), (1, 2, LAST)]
                    for a0, a1, w in spans:
                        j0, j1 = 2 * q + a0, 2 * q + a1
                        o = ov[0:w, a0:a1]
                        dn = den[0:w, a0:a1, :]
                        ao = xt[0:w, j0:j1, :].rearrange("p j (h d) -> p j h d", d=DH)
                        shape = [w, a1 - a0, H, DH]
                        v.tensor_tensor(dn, o[:, :, :, DH], sself[0:w, j0:j1, :], ALU.add)
                        link(v.tensor_tensor(ao, V[0:w, j0:j1, :, 0:DH],
                                                sself[0:w, j0:j1, :].unsqueeze(3).to_broadcast(shape), ALU.mult))
                        v.reciprocal(dn, dn)
                        ins = v.tensor_tensor(ao, o[:, :, :, 0:DH], ao, ALU.add)
                        if a1 == 2:
                            ins.then_inc(free[SLOT[f"oT{q}"]], 1)
                            v.wait_ge(free[SLOT[f"oT{q}"]], freed(i, f"oT{q}"))
                        else:
                            link(ins)
                        ins = v.tensor_tensor(ao, ao, dn.unsqueeze(3).to_broadcast(shape), ALU.mult)
                        if a1 == 2:
                            ins.then_inc(ao_ready, 1)
                            v.wait_ge(ao_ready, at(i, "ao_ready", q + 1))
                        else:
                            link(ins)
                v.wait_ge(h_summed, at(i, "h_summed", 2))
                add_to_h("att")

                layernorm(3)
                v.wait_ge(full[SLOT["tree"]], filled(i, "tree"))
                ins = v.tensor_copy(tl[:, :, :], slot("tree")[:, 0, 0:NT * NODES].rearrange("p (j n) -> p j n", n=NODES))
                ins.then_inc(free[SLOT["tree"]], 1)
                v.wait_ge(free[SLOT["tree"]], freed(i, "tree"))
                v.tensor_scalar(tc[:, :, :], tl[:, :, :], 0.0, None, ALU.is_gt).then_inc(tree_ready, 1)
                v.wait_ge(tree_ready, at(i, "tree_ready", 1))
                v.tensor_copy(ta[:, :, 2], tc[:, :, 0])
                link(v.tensor_scalar(ta[:, :, 1], tc[:, :, 0], -1.0, 1.0, ALU.mult, ALU.add))
                for a0, a1 in ((1, 3), (3, 7), (7, 10)):
                    right = ta[:, :, 2 * a0 + 2:2 * a1 + 1:2]
                    link(v.tensor_tensor(right, ta[:, :, a0:a1], tc[:, :, a0:a1], ALU.mult))
                    link(v.tensor_tensor(ta[:, :, 2 * a0 + 1:2 * a1:2], ta[:, :, a0:a1], right, ALU.subtract))
                link(v.tensor_reduce(tsum[:, :], ta[:, :, 10:15], AX.X, ALU.add))
                link(v.tensor_tensor(ta[:, :, 20], ta[:, :, 20], tsum[:, :], ALU.add))
                v.wait_ge(tree_gelu, at(i, "tree_gelu", 1))
                link(v.tensor_tensor(tl[:, :, :], ta[:, :, :], te[:, :, :], ALU.mult))
                link(v.tensor_tensor(tc[:, :, 0:10], tc[:, :, 0:10], tl[:, :, 0:10], ALU.mult))
                v.tensor_copy(cf[:, :, 2:21:2], tc[:, :, 0:10])
                v.tensor_tensor(cf[:, :, 1:20:2], tl[:, :, 0:10], tc[:, :, 0:10], ALU.subtract)
                v.memset(cf[:, :, 0], 0.0)
                link(v.tensor_reduce(tsum[:, :], tl[:, :, 10:21], AX.X, ALU.add))
                link(v.tensor_tensor(cf[:, :, 20], cf[:, :, 20], tsum[:, :], ALU.add))
                v.scalar_tensor_tensor(cf[:, :, 20], te[:, :, 20], float(DEPTH - 1 - 5), cf[:, :, 20], ALU.mult, ALU.add).then_inc(coef_ready, 1)
                add_to_h("out", h, xt)
                assert links[0] == COUNTS["dve_chain"], links

        @block.tensor
        def _(t):
            def transpose_blocks(n):
                for x in range(14 * (n % 2), 14 * (n % 2) + (13 if n == 1 else 14)):
                    src = px1[:, x, :] if n >= 2 else px2[:, x:x + 2, :].rearrange("y e n -> y (e n)")
                    ins = t.transpose(ACC[:, n % 2, NY * (x % 14):NY * (x % 14) + NY], src, ident[0:NY, 0:NY])
                return ins

            BLOCKS_AT, TAPS_AT = 4, NT * H - 2 * 4 * 6
            TAPS = 6

            def patch_product(n, tap):
                m, c = divmod(n, 2)
                y0, ny = 14 * c, 14 - c
                o = ACC[0:KD, c, 0:ny * OUT].rearrange("p (y x) -> p y x", x=OUT)
                cols = slice(KD * m, KD * m + KD)
                if tap < 4:
                    a, e = divmod(tap, 2)
                    return t.matmul(o, lhsT=w_tok1[:, tap, cols], rhs=bl1[:, y0 + a:y0 + a + ny, e:e + OUT],
                                    start=tap == 0, stop=False)
                a = tap - 4
                return t.matmul(o, lhsT=w_tok2[:, a, cols], rhs=bl2[:, y0 + a:y0 + a + ny, 0:OUT],
                                start=False, stop=tap == TAPS - 1)

            t.wait_ge(pixels_sorted, 2)
            for n in range(4):
                if n >= 2:
                    t.wait_ge(front_taken, n - 1)
                    t.sem_inc(waits_apart, 1)
                transpose_blocks(n).then_inc(front_done, 1)
            t.wait_ge(front_taken, 4)
            for n in range(4):
                if n >= 2:
                    t.wait_ge(front_taken, n + 3)
                for tap in range(TAPS):
                    ins = patch_product(n, tap)
                ins.then_inc(front_done, 1)
            t.wait_ge(front_taken, 8)
            with t.Fori(0, B) as i:

                def feature_major(job, n, terms):
                    t.wait_ge(free[SLOT[job]], vacant(i, job))
                    for c in range(2):
                        for k, (lhsT, rhs) in enumerate(terms):
                            ins = t.matmul(slot(job)[0:n, c, 0:CW], lhsT=lhsT, rhs=rhs[:, c * CW:(c + 1) * CW],
                                           start=k == 0, stop=k == len(terms) - 1)
                    ins.then_inc(full[SLOT[job]], 1)

                def token_major(job, j0, nj, terms):
                    t.wait_ge(free[SLOT[job]], vacant(i, job))
                    for j in range(nj):
                        for k, (lhsT, rhs) in enumerate(terms):
                            ins = t.matmul(slot(job)[:, j // 2, D * (j % 2):D * (j % 2) + D],
                                           lhsT=lhsT[:, 128 * (j0 + j):128 * (j0 + j) + 128], rhs=rhs,
                                           start=k == 0, stop=k == len(terms) - 1)
                    ins.then_inc(full[SLOT[job]], 1)

                def transposes(name, src):
                    for m in range(2):
                        t.wait_ge(free[SLOT[f"{name}{m}"]], vacant(i, f"{name}{m}"))
                        for j in range(NT):
                            ins = t.transpose(flat(f"{name}{m}")[0:KD, 128 * j:128 * j + 128],
                                              src[:, j, KD * m:KD * m + KD], ident[:, :])
                        ins.then_inc(full[SLOT[f"{name}{m}"]], 1)

                for q, (j0, nj) in enumerate(HALVES):
                    t.wait_ge(free[SLOT[f"emb{q}"]], vacant(i, f"emb{q}"))
                    for m in range(2):
                        for j in range(nj):
                            ins = t.transpose(slot(f"emb{q}")[:, j // 2, D * (j % 2) + KD * m:D * (j % 2) + KD * m + KD],
                                              tokT[:, m, 128 * (j0 + j):128 * (j0 + j) + 128], ident[0:KD, 0:KD])
                    ins.then_inc(full[SLOT[f"emb{q}"]], 1)

                def half_ready(name):
                    t.wait_ge(free[SLOT[f"{name}0"]], freed(i, f"{name}0"))
                    t.wait_ge(free[SLOT[f"{name}1"]], freed(i, f"{name}1"))

                t.wait_ge(xn_ready, at(i, "xn_ready", 1))
                transposes("xnT", xn)
                half_ready("xnT")
                for m in range(2 * ND):
                    feature_major(f"xz{m}", 128, [(w_in[:, k, 128 * m:128 * m + 128], xT[:, k, :]) for k in range(2)])
                t.wait_ge(u_ready, at(i, "u_ready", 3))
                feature_major("proj", KD, [(w_x[:, m, :], u[:, m, :]) for m in range(ND)])
                t.wait_ge(free[SLOT["proj"]], freed(i, "proj"))
                for m in range(ND):
                    feature_major(f"dt{m}", 128, [(w_dt[:, 128 * m:128 * m + 128], prT[:, :])])
                for k, job in enumerate(("B0", "C0")):
                    feature_major(job, 128, [(sel_b[:, k, :], prT[:, :])])
                t.wait_ge(bc_ready, at(i, "bc_ready", 1))
                t.wait_ge(free[SLOT["BC15"]], vacant(i, "BC15"))
                for k, bd in enumerate((bdB, bdC)):
                    ins = t.matmul(slot("BC15")[:, k, 0:NG * LS], lhsT=ones[0:KD, 0:128], rhs=bd, start=True, stop=True)
                ins.then_inc(full[SLOT["BC15"]], 1)
                t.wait_ge(tail_flag, at(i, "tail_flag", 1))
                t.sem_inc(waits_apart, 1)
                with t.If(t.value_load(flag[0:1, 0:1]) != 0):
                    for n in range(NG):
                        if n > 0:
                            t.wait_ge(tail_used, at(i, "tail_used", n))
                        for bank, row in ((6, BROW + 1 + n), (0, CROW + 1 + n)):
                            for c in range(2):
                                ins = t.matmul(PS[:, bank + c, 0:CW], lhsT=ident[0:KD, row:row + 1].to_broadcast([KD, 128]),
                                               rhs=prT[:, c * CW:(c + 1) * CW], start=True, stop=True)
                        ins.then_inc(tail_bc, 1)
                with t.Else():
                    t.sem_inc(tail_bc, COUNTS["tail_bc"])
                t.wait_ge(gated_ready, at(i, "gated_ready", 1))
                for q, (j0, nj) in enumerate(HALVES):
                    token_major(f"mix{q}", j0, nj, [(gated[:, m, :], w_out[:, m, :]) for m in range(ND)])

                t.wait_ge(norm_ready, at(i, "norm_ready", 2))
                transposes("x2T", xt)
                half_ready("x2T")
                t.wait_ge(free[SLOT["route"]], vacant(i, "route"))
                for j in range(NT):
                    for m in range(2):
                        ins = t.matmul(slot("route")[:, 0, E * j:E * j + E], lhsT=xT[:, m, 128 * j:128 * j + 128],
                                       rhs=w_route[:, m, :], start=m == 0, stop=m == 1)
                ins.then_inc(full[SLOT["route"]], 1)
                t.wait_ge(hot_ready, at(i, "hot_ready", 1))
                t.wait_ge(free[SLOT["hotT"]], vacant(i, "hotT"))
                for j in range(NT):
                    ins = t.transpose(flat("hotT")[0:E, 128 * j:128 * j + 128], hot[:, j, :], ident[:, :])
                ins.then_inc(full[SLOT["hotT"]], 1)
                for m in range(4):
                    feature_major(f"hid{m}", 128, [(w_1[:, k, 128 * m:128 * m + 128], xT[:, k, :]) for k in range(2)])
                    if m == 0:
                        t.wait_ge(free[SLOT["hotT"]], freed(i, "hotT"))
                    feature_major(f"mask{m}", 128, [(sel_e[:, m, :], hotT[:, :])])
                for m in range(4):
                    t.wait_ge(free[SLOT[f"mask{m}"]], freed(i, f"mask{m}"))
                for q, (j0, nj) in enumerate(HALVES):
                    token_major(f"ffn{q}", j0, nj, [(gated[:, m, :], w_2[:, m, :]) for m in range(4)]
                                + [(hotT[:, :], b_2[:, k, :]) for k in range(3)])

                t.wait_ge(norm_ready, at(i, "norm_ready", 3))
                transposes("x3T", xt)
                half_ready("x3T")
                for k, job in enumerate(("q0", "q1", "k0", "k1")):
                    feature_major(job, KD, [(w_qkv[:, n, KD * k:KD * k + KD], xT[:, n, :]) for n in range(2)])
                for q, (j0, nj) in enumerate(HALVES):
                    token_major(f"v{q}", j0, nj, [(xT[:, n, :], w_qkv[:, n, 2 * D:3 * D]) for n in range(2)])
                t.wait_ge(selfprod_ready, at(i, "selfprod_ready", 2))
                t.wait_ge(free[SLOT["self"]], vacant(i, "self"))
                for j in range(NT):
                    w = width(j)
                    for m in range(2):
                        ins = t.matmul(slot("self")[0:w, 0, H * j:H * j + H], lhsT=prod[0:KD, 4 + m, 128 * j:128 * j + w],
                                       rhs=self_w[:, m, :], start=m == 0, stop=m == 1)
                ins.then_inc(full[SLOT["self"]], 1)

                def without_diagonal(job, w, j, starts, n_rows, left, right):
                    t.wait_ge(free[SLOT[job]], vacant(i, job))
                    for c, c0 in enumerate(starts):
                        lo, hi = max(128 * j, c0), min(128 * j + w, c0 + CW)
                        t_ins = t.matmul(slot(job)[0:w, c, 0:CW], lhsT=left[0:n_rows, 128 * j:128 * j + w],
                                         rhs=right[0:n_rows, c0:c0 + CW], start=True, stop=lo >= hi)
                        if lo < hi:
                            t_ins = t.matmul(slot(job)[0:w, c, lo - c0:hi - c0], lhsT=identb[0:w, 0:w],
                                             rhs=negbig[0:w, lo - 128 * j:hi - 128 * j], start=False, stop=True)
                    t_ins.then_inc(full[SLOT[job]], 1)

                t.wait_ge(stack_in, at(i, "stack_in", 192))
                for hd in range(H):
                    for j in range(NT):
                        without_diagonal(f"S{hd}_{j}", width(j), j, (0, T - CW), KD, Qs[:, hd, :], Ks[:, hd, :])
                        n = hd * NT + j - BLOCKS_AT
                        if n >= 0 and n % 4 == 0 and n < 16:
                            n //= 4
                            t.wait_ge(pixels_sorted, at(i, "pixels_sorted", 1 + n // 2))
                            if n >= 2:
                                t.wait_ge(front_taken, at(i, "front_taken", n - 1))
                            t.sem_inc(waits_apart, 1)
                            transpose_blocks(n).then_inc(front_done, 1)
                        n = hd * NT + j - TAPS_AT
                        if n >= 0 and n % 2 == 0:
                            n, tap = divmod(n // 2, TAPS)
                            if tap == 0:
                                t.wait_ge(front_taken, at(i, "front_taken", 4 if n < 2 else n + 3))
                            ins = patch_product(n, tap)
                            if tap == TAPS - 1:
                                ins.then_inc(front_done, 1)
                t.wait_ge(shift_ready, at(i, "shift_ready", 1))
                for n in range(2):
                    t.wait_ge(free[SLOT[f"shiftT{n}"]], vacant(i, f"shiftT{n}"))
                    for j in range(NT):
                        ins = t.transpose(flat(f"shiftT{n}")[0:H, 128 * j:128 * j + 128], shift[:, n, j, :], ident[:, :])
                    ins.then_inc(full[SLOT[f"shiftT{n}"]], 1)
                t.wait_ge(shift_in, at(i, "shift_in", 32))
                t.wait_ge(ones_ready, at(i, "ones_ready", 1))

                def weigh(n):
                    g, j = divmod(n, NT)
                    w = width(j)
                    if j == 0 and g > 0:
                        t.wait_ge(pv_taken, at(i, "pv_taken", g))
                    if n == 0:
                        t.wait_ge(front_taken, at(i, "front_taken", 8))
                    t.wait_ge(free[SLOT[f"ST{4 * g + 3}_{j}"]], freed(i, f"ST{4 * g + 3}_{j}"))
                    for c in range(2):
                        for hh in range(4):
                            ins = t.matmul(ACC[32 * hh:32 * hh + 32, c, 0:CW], lhsT=V[0:w, j, 4 * g + hh, :],
                                           rhs=PT[0:w, 4 * (n % 2) + hh, c * CW:(c + 1) * CW],
                                           start=j == 0, stop=j == NT - 1, tile_position=(0, 32 * hh))
                    ins.then_inc(pv_done, 1)

                for n in range(3 * NT):
                    g, j = divmod(n, NT)
                    for hd in range(4 * g, 4 * g + 4):
                        without_diagonal(f"ST{hd}_{j}", width(j), j, (0, CW), KD + 2, Ks[:, hd, :], Qs[:, hd, :])
                    if n > 0:
                        weigh(n - 1)
                weigh(3 * NT - 1)
                for q in range(3):
                    t.wait_ge(free[SLOT[f"oT{q}"]], vacant(i, f"oT{q}"))
                    if q == 0:
                        t.wait_ge(pv_taken, at(i, "pv_taken", 3))
                    for j in range(2):
                        for g in range(3):
                            ins = t.transpose(slot(f"oT{q}")[:, j, 128 * g:128 * g + 128],
                                              OT[:, g, 128 * (2 * q + j):128 * (2 * q + j) + 128], ident[:, :])
                    ins.then_inc(full[SLOT[f"oT{q}"]], 1)
                t.wait_ge(ao_ready, at(i, "ao_ready", 3))
                transposes("aoT", xt)
                half_ready("aoT")
                for q, (j0, nj) in enumerate(HALVES):
                    token_major(f"att{q}", j0, nj, [(xT[:, k, :], w_pr[:, k, :]) for k in range(2)])

                t.wait_ge(norm_ready, at(i, "norm_ready", 4))
                transposes("x4T", xt)
                half_ready("x4T")
                t.wait_ge(free[SLOT["tree"]], vacant(i, "tree"))
                for j in range(NT):
                    for m in range(2):
                        ins = t.matmul(slot("tree")[:, 0, NODES * j:NODES * j + NODES], lhsT=xT[:, m, 128 * j:128 * j + 128],
                                       rhs=w_tree[:, m, :], start=m == 0, stop=m == 1)
                ins.then_inc(full[SLOT["tree"]], 1)
                t.wait_ge(coef_ready, at(i, "coef_ready", 1))
                t.wait_ge(free[SLOT["coefT"]], vacant(i, "coefT"))
                for j in range(NT):
                    ins = t.transpose(flat("coefT")[0:NODES, 128 * j:128 * j + 128], cf[:, j, :], ident[:, :])
                ins.then_inc(full[SLOT["coefT"]], 1)
                t.wait_ge(free[SLOT["coefT"]], freed(i, "coefT"))
                for q, (j0, nj) in enumerate(HALVES):
                    token_major(f"out{q}", j0, nj, [(coefT[:, :], w_leaf[:, :])])



_INS = ["x", "cls_tok", "L0_tok_w", "L0_tok_b", "L0_tok_cls_token", "L0_tok_pos_embedding", "L0_attn_w_norm",
        "L0_attn_w_in", "L0_attn_conv_w", "L0_attn_conv_b", "L0_attn_w_xproj", "L0_attn_w_dt", "L0_attn_b_dt",
        "L0_attn_A_log", "L0_attn_D_param", "L0_attn_w_out", "L0_ffn_enc_w", "L0_ffn_enc_b", "L0_ffn_sw_w",
        "L0_ffn_sw_b", "L0_ffn_w1", "L0_ffn_b1", "L0_ffn_w2", "L0_ffn_b2", "L1_attn_w_qkv", "L1_attn_w_proj",
        "L1_attn_b_proj", "L1_attn_temperature", "L1_ffn_weights_in", "L1_ffn_weights_out"]


def kernel(**inputs):
    import concourse.bacc as bacc
    from concourse.bass_utils import run_bass_kernel_spmd

    nc = bacc.Bacc("TRN2", target_bir_lowering=False, num_devices=1)
    arrays, ap = {}, {}
    for name in _INS:
        a = np.ascontiguousarray(inputs[name])
        arrays[f"in_{name}"] = a
        ap[name] = nc.dram_tensor(f"in_{name}", a.shape, mybir.dt.from_np(a.dtype), kind="ExternalInput").ap()
    out = nc.dram_tensor("out", (B, T, D), F32, kind="ExternalOutput").ap()
    tower(nc, ap, out)
    return run_bass_kernel_spmd(nc, [arrays], core_ids=[0]).results[0]["out"]
```

```python
from contextlib import ExitStack

import numpy as np

import concourse.bass as bass
from concourse import mybir

F32 = mybir.dt.float32
BF16 = mybir.dt.bfloat16
I32 = mybir.dt.int32
ALU = mybir.AluOpType
ACT = mybir.ActivationFunctionType
AX = mybir.AxisListType

B, C, IMG = 32, 3, 224
P, S = 16, 8
NY = IMG // S
OUT = (IMG - P) // S + 1
T = OUT * OUT + 2
D = 192
KD = 96
NT = (T + 127) // 128
LAST = T - 128 * (NT - 1)
TW = NT * 128
CW = (T + 1) // 2
T2 = 2 * CW
DI, ND = 384, 3
NS, RANK = 16, 24
BROW, CROW = 32, 64
LS = 24
NG = NS - 1
E, R = 8, 64
H, DH = 12, 16
DEPTH = 11
NODES = 2 * DEPTH - 1
EPS = 1e-5
BIG = 1e30
CLAMP, LOW = 20.0, -7.0
DEAD = -104.0
HALVES = [(0, 4), (4, 2)]

GROUPS, GH = 3, 4
STEPS = GROUPS * NT
S_JOBS = H * NT
S_GROUP = GH * NT
S_FIRST = S_GROUP + 8
SHIFT0_AT = S_GROUP + 2
SHIFT_AT = {4: 1, 10: 2}
OT_AT = {10: 0, 13: 1}
OT_TAKEN_AT = S_FIRST + GH * 7 + 1


def attention_jobs():
    names = [f"S{s // NT}_{s % NT}" for s in range(SHIFT0_AT)] + ["shift0"]
    names += [f"S{s // NT}_{s % NT}" for s in range(SHIFT0_AT, S_FIRST)]
    s = S_FIRST
    for n in range(STEPS):
        for hh in range(GH):
            names.append(f"ST{GH * (n // NT) + hh}_{n % NT}")
            if s < S_JOBS:
                names.append(f"S{s // NT}_{s % NT}")
                s += 1
        if n in SHIFT_AT:
            names.append(f"shift{SHIFT_AT[n]}")
        if n in OT_AT:
            names.append(f"oT{OT_AT[n]}")
    return names + ["oT2"]


JOBS = (["xnT0", "xnT1"]
        + [f"xz{m}" for m in range(6)] + ["proj"] + [f"dt{m}" for m in range(ND)]
        + ["B0", "BC15", "mix0", "mix1"]
        + ["x2T0", "x2T1", "route"] + ["hid0", "hid1", "hotT", "hid2", "mask0", "mask1", "hid3", "mask2", "mask3"]
        + ["ffn0", "ffn1"]
        + ["x3T0", "x3T1", "q0", "q1", "k0", "k1", "v0", "v1", "self"]
        + attention_jobs() + ["aoT0", "aoT1", "att0", "att1"]
        + ["x4T0", "x4T1", "tree", "emb0", "emb1", "coefT", "out0", "out1"])
SLOTS = 3
SLOT = {name: n % SLOTS for n, name in enumerate(JOBS)}
TURN = {name: n // SLOTS for n, name in enumerate(JOBS)}
TURNS = [sum(s == k for s in SLOT.values()) for k in range(SLOTS)]

COUNTS = dict(
    dve_chain=79, pool_chain=7,
    pixels_in=16, pixels_sorted=2, front_done=8, front_taken=8,
    emb_stats_ready=1, emb_rstd_ready=1, stats_ready=3, rstd_ready=3, xn_ready=6, norm_ready=24, h_summed=2, 
    conv_ready=3, u_ready=3, pre_ready=3, exp3_ready=1, soft_ready=3,
    delta_ready=3, c_rows_ready=1, c_rows_taken=1, cz_ready=3, du_ready=3, ud_ready=3, udz_ready=3, decay_log_ready=3, decays_ready=3, bc_ready=1, log15_ready=1, decays15_ready=1,
    gated15_ready=1, gated_ready=1, end_ready=1, alive_ready=1, hot_ready=1, exp_ready=1, logits_ready=1,
    parts1_ready=4, rest_ready=4, parts2_ready=4, split_ready=4,
    selfprod_ready=2, shift_ready=3, ones_ready=1,
    q_parts_out=32, k_parts_out=32, stack_in=192, stack_rest_in=192, shift_out=48, shift_in=48, pv_done=18, pv_taken=3,
    self_exp=3, ao_ready=3, tree_ready=1, tree_gelu=1, coef_ready=1, 
    out_stored=32,
)


AHEAD = {"pixels_in": 16, "pixels_sorted": 2, "front_done": 8, "front_taken": 8, "emb_stats_ready": 1, "emb_rstd_ready": 1, "out_stored": 1}
PSUM_AHEAD = 1
TAIL_STEPS = 20
COUNTS.update(tail_flag=1, tail_bc=NG, tail_log=ND * NG, tail_exp=ND * NG, tail_used=NG, tail_chain=NG * TAIL_STEPS)


def at(i, name, k):
    return i * COUNTS[name] + (k + AHEAD.get(name, 0))


def vacant(i, job):
    return i * TURNS[SLOT[job]] + (TURN[job] + PSUM_AHEAD)


def filled(i, job):
    return i * TURNS[SLOT[job]] + (TURN[job] + 1)


def freed(i, job):
    return i * TURNS[SLOT[job]] + (TURN[job] + 1 + PSUM_AHEAD)


def tower(nc, ap, out):
    ctx = ExitStack()
    with ctx:
        def sb(name, shape, dt=F32):
            return ctx.enter_context(nc.sbuf_tensor(name, shape, dt))

        dve_chain = ctx.enter_context(nc.semaphore("dve_chain"))
        pool_chain = ctx.enter_context(nc.semaphore("pool_chain"))
        pixels_in = ctx.enter_context(nc.semaphore("pixels_in"))
        pixels_sorted = ctx.enter_context(nc.semaphore("pixels_sorted"))
        front_done = ctx.enter_context(nc.semaphore("front_done"))
        front_taken = ctx.enter_context(nc.semaphore("front_taken"))
        emb_stats_ready = ctx.enter_context(nc.semaphore("emb_stats_ready"))
        emb_rstd_ready = ctx.enter_context(nc.semaphore("emb_rstd_ready"))
        first_emb_full = ctx.enter_context(nc.semaphore("first_emb_full"))
        first_emb_read = ctx.enter_context(nc.semaphore("first_emb_read"))
        first_emb = ctx.enter_context(nc.semaphore("first_image_embedded"))
        stats_ready = ctx.enter_context(nc.semaphore("stats_ready"))
        rstd_ready = ctx.enter_context(nc.semaphore("rstd_ready"))
        norm_ready = ctx.enter_context(nc.semaphore("norm_ready"))
        h_summed = ctx.enter_context(nc.semaphore("h_summed"))
        xn_ready = ctx.enter_context(nc.semaphore("xn_ready"))
        conv_ready = ctx.enter_context(nc.semaphore("conv_ready"))
        u_ready = ctx.enter_context(nc.semaphore("u_ready"))
        pre_ready = ctx.enter_context(nc.semaphore("pre_ready"))
        exp3_ready = ctx.enter_context(nc.semaphore("exp3_ready"))
        soft_ready = ctx.enter_context(nc.semaphore("soft_ready"))
        delta_ready = ctx.enter_context(nc.semaphore("delta_ready"))
        c_rows_ready = ctx.enter_context(nc.semaphore("c_rows_ready"))
        c_rows_taken = ctx.enter_context(nc.semaphore("c_rows_taken"))
        cz_ready = ctx.enter_context(nc.semaphore("cz_ready"))
        ud_ready = ctx.enter_context(nc.semaphore("ud_ready"))
        udz_ready = ctx.enter_context(nc.semaphore("udz_ready"))
        du_ready = ctx.enter_context(nc.semaphore("du_ready"))
        decay_log_ready = ctx.enter_context(nc.semaphore("decay_log_ready"))
        decays_ready = ctx.enter_context(nc.semaphore("decays_ready"))
        bc_ready = ctx.enter_context(nc.semaphore("bc_ready"))
        log15_ready = ctx.enter_context(nc.semaphore("log15_ready"))
        decays15_ready = ctx.enter_context(nc.semaphore("decays15_ready"))
        gated15_ready = ctx.enter_context(nc.semaphore("gated15_ready"))
        gated_ready = ctx.enter_context(nc.semaphore("gated_ready"))
        end_ready = ctx.enter_context(nc.semaphore("end_ready"))
        alive_ready = ctx.enter_context(nc.semaphore("alive_ready"))
        hot_ready = ctx.enter_context(nc.semaphore("hot_ready"))
        exp_ready = ctx.enter_context(nc.semaphore("exp_ready"))
        logits_ready = ctx.enter_context(nc.semaphore("logits_ready"))
        parts1_ready = ctx.enter_context(nc.semaphore("parts1_ready"))
        rest_ready = ctx.enter_context(nc.semaphore("rest_ready"))
        parts2_ready = ctx.enter_context(nc.semaphore("parts2_ready"))
        split_ready = ctx.enter_context(nc.semaphore("split_ready"))
        selfprod_ready = ctx.enter_context(nc.semaphore("selfprod_ready"))
        shift_ready = ctx.enter_context(nc.semaphore("shift_ready"))
        ones_ready = ctx.enter_context(nc.semaphore("ones_ready"))
        q_parts_out = ctx.enter_context(nc.semaphore("q_parts_out"))
        k_parts_out = ctx.enter_context(nc.semaphore("k_parts_out"))
        stack_in = ctx.enter_context(nc.semaphore("stack_in"))
        stack_rest_in = ctx.enter_context(nc.semaphore("stack_rest_in"))
        shift_out = ctx.enter_context(nc.semaphore("shift_out"))
        shift_in = ctx.enter_context(nc.semaphore("shift_in"))
        pv_done = ctx.enter_context(nc.semaphore("pv_done"))
        pv_taken = ctx.enter_context(nc.semaphore("pv_taken"))
        self_exp = ctx.enter_context(nc.semaphore("self_exp"))
        ao_ready = ctx.enter_context(nc.semaphore("ao_ready"))
        tree_ready = ctx.enter_context(nc.semaphore("tree_ready"))
        tree_gelu = ctx.enter_context(nc.semaphore("tree_gelu"))
        coef_ready = ctx.enter_context(nc.semaphore("coef_ready"))
        out_stored = ctx.enter_context(nc.semaphore("out_stored"))
        tail_flag = ctx.enter_context(nc.semaphore("tail_flag"))
        tail_bc = ctx.enter_context(nc.semaphore("tail_bc"))
        tail_log = ctx.enter_context(nc.semaphore("tail_log"))
        tail_exp = ctx.enter_context(nc.semaphore("tail_exp"))
        tail_used = ctx.enter_context(nc.semaphore("tail_used"))
        tail_chain = ctx.enter_context(nc.semaphore("tail_chain"))
        full = [ctx.enter_context(nc.semaphore(f"psum_full{k}")) for k in range(SLOTS)]
        free = [ctx.enter_context(nc.semaphore(f"psum_free{k}")) for k in range(SLOTS)]
        s_w = ctx.enter_context(nc.semaphore("weights_in"))
        s_setup_v = ctx.enter_context(nc.semaphore("setup_vector"))
        s_setup_g = ctx.enter_context(nc.semaphore("setup_gpsimd"))
        s_setup_a = ctx.enter_context(nc.semaphore("setup_scalar"))
        s_setup_t = ctx.enter_context(nc.semaphore("setup_tensor"))

        PS = ctx.enter_context(nc.psum_tensor("PS", [128, 8, 512], F32))
        ACC = PS[:, 6:8, :]

        def slot(name):
            return PS[:, 2 * SLOT[name]:2 * SLOT[name] + 2, :]

        def wide(name, n=128):
            return slot(name)[0:n, :, 0:CW]

        ident = sb("ident", [128, 128])
        identb = sb("identb", [128, 128], BF16)
        negbig = sb("negbig", [128, 128], BF16)
        ones = sb("ones", [128, 128])
        onesb = sb("onesb", [128, T2], BF16)
        first15 = sb("first15", [128, ND * NG * LS], BF16)
        warm = sb("warm", [128, 4])
        clamp = sb("clamp", [128, 1])
        minus_half2 = sb("minus_half2", [128, 2, NT])
        minus_half = minus_half2[:, 0, :]
        rank8 = sb("rank8", [128, NT, E])
        w_tok1 = sb("w_tok1", [128, 4, D])
        w_tok2 = sb("w_tok2", [128, 2, D])
        base = sb("base", [128, NT, D])
        w_in = sb("w_in", [KD, 2, 2 * DI])
        w_norm = sb("w_norm", [KD, 2])
        conv_w = sb("conv_w", [128, ND, 4])
        conv_b = sb("conv_b", [128, ND])
        w_x = sb("w_x", [128, ND, KD])
        w_dt = sb("w_dt", [KD, DI])
        b_dt = sb("b_dt", [128, ND])
        Aneg = sb("Aneg", [128, ND, NS])
        Dp = sb("Dp", [128, ND])
        w_out = sb("w_out", [128, ND, D])
        sel_b = sb("sel_b", [KD, 2, 128])
        w_route = sb("w_route", [KD, 2, E])
        b_route = sb("b_route", [128, E])
        w_1 = sb("w_1", [KD, 2, E * R])
        b_1 = sb("b_1", [128, 4])
        w_2 = sb("w_2", [128, 4, D])
        b_2 = sb("b_2", [KD, 3, D], BF16)
        sel_e = sb("sel_e", [KD, 4, 128], BF16)
        w_qkv = sb("w_qkv", [KD, 2, 3 * D])
        self_w = sb("self_w", [KD, 2, H])
        w_pr = sb("w_pr", [KD, 2, D])
        b_pr = sb("b_pr", [128, D])
        w_tree = sb("w_tree", [KD, 2, NODES])
        w_leaf = sb("w_leaf", [KD, D])

        xin = sb("xin", [NY, C * 8, IMG])
        bl1 = sb("bl1", [128, NY, NY])
        bl2 = sb("bl2", [128, NY, NY])
        h = sb("h", [128, NT, D])
        xt = sb("xt", [128, NT, D])
        xT = sb("xT", [KD, 2, TW])
        st = sb("st", [128, NT, 6])
        mv = sb("mv", [128, NT, 2])
        rs = sb("rs", [128, 2, NT])
        est = sb("est", [128, NT, 6])
        emv = sb("emv", [128, NT, 2])
        ers = sb("ers", [128, 4, NT])
        prT = sb("prT", [KD, TW])
        gated = sb("gated", [128, 4, TW])
        tokT = gated[0:KD, 0:2, :]
        arena = sb("arena", [128, 14640])
        def rows(k):
            return arena[:, k * ND * TW:(k + 1) * ND * TW].rearrange("p (m t) -> p m t", m=ND)
        u, zs, dl, du, gg, lw = (rows(k) for k in range(6))
        xi = gg
        PT = arena[:, 0:8 * T2].rearrange("p (b t) -> p b t", b=8)
        Qs = arena[:, 8 * T2:14 * T2].bitcast(BF16).rearrange("p (h t) -> p h t", h=H)
        Ks = arena[:, 14 * T2:20 * T2].bitcast(BF16).rearrange("p (h t) -> p h t", h=H)
        qkf = sb("qkf", [128, 4, T2])
        xn = qkf[:, 0:2, :].rearrange("p a t -> p (a t)")[:, 0:NT * D].rearrange("p (j d) -> p j d", j=NT)
        emb = qkf[:, 2:4, :].rearrange("p a t -> p (a t)")[:, 0:NT * D].rearrange("p (j d) -> p j d", j=NT)
        cz = qkf[:, 0:3, :]
        Cs = arena[:, 6 * ND * TW:6 * ND * TW + T2]
        Bs = qkf[:, 3, :]
        OT = qkf[:, :, :].rearrange("p a t -> p (a t)")[:, 0:3 * TW].rearrange("p (g t) -> p g t", g=3)
        parts_f = sb("parts_f", [128, 6 * T2])
        parts = parts_f[0:KD, :].bitcast(BF16).rearrange("p (w i m t) -> p w i m t", w=2, i=3, m=2)
        def small(k):
            return parts_f[:, k * ND * NG * LS:(k + 1) * ND * NG * LS]
        g15, l15, x15, s15 = (small(k) for k in range(4))
        bdB = xT[:, 0, 0:NG * LS]
        bdC = xT[:, 1, 0:NG * LS]
        rest = PT
        prod = PT
        ends15 = sb("ends15", [128, 2, ND, NG])
        alive = sb("alive", [128, 2])
        flag = sb("flag", [128, 1], I32)
        logit = sb("logit", [128, NT, E])
        hot = sb("hot", [128, NT, E])
        best = sb("best", [128, 4, NT])
        hotT = sb("hotT", [KD, TW], BF16)
        V = sb("V", [128, NT, H, 32])
        smax = sb("smax", [128, H, NT])
        smid = sb("smid", [128, NT, H])
        sself = sb("sself", [128, NT, H])
        shift = sb("shift", [128, NT, GROUPS, 2 * GH])
        stot = sb("stot", [128, NT, H])
        shiftT = sb("shiftT", [2 * GH, 2, T2], BF16)
        den = sb("den", [128, NT, GH])
        tl = sb("tl", [128, NT, NODES])
        tc = sb("tc", [128, NT, NODES])
        ta = sb("ta", [128, NT, NODES])
        te = sb("te", [128, NT, NODES])
        cf = sb("cf", [128, NT, NODES])
        tsum = sb("tsum", [128, NT])
        mb = sb("mb", [128, 2, NT, H], BF16)
        coefT = prT

        scr_qk = nc.dram_tensor("scr_qk", (2, 3, D, T2), BF16).ap()
        scr_shift = nc.dram_tensor("scr_shift", (GROUPS, 2 * GH, T2), BF16).ap()

        wp = arena[0:KD, 3000:4024].rearrange("p (m k x) -> p m k x", m=2, k=4)
        wp2 = arena[0:KD, 4024:4536].rearrange("p (m k x) -> p m k x", m=2, k=4)
        px = arena[0:NY, 8 * T2:8 * T2 + NY * 192]
        px1 = px[:, 0:NY * 128].rearrange("y (x n) -> y x n", n=128)
        px2 = px[:, NY * 128:].rearrange("y (x n) -> y x n", n=64)
        n_w = [0]

        with nc.Block() as block:
            @block.sync
            def _(sp):
                def load(dst, src, slow=False):
                    sp.dma_start(dst, src, allow_slow_non_contiguous=slow).then_inc(s_w, 16)
                    n_w[0] += 16
                sp.wait_ge(s_setup_v, 1)
                load(arena[0:KD, 0:1536].rearrange("p (m k) -> p m k", m=2),
                     ap["L0_tok_w"].rearrange("(m p) k -> p m k", p=KD))
                load(arena[0:KD, 1536:1664].rearrange("p (m r) -> p m r", m=2),
                     ap["L0_ffn_enc_w"].rearrange("(m p) r -> p m r", p=KD))
                load(arena[0:R, 1664:1672], ap["L0_ffn_sw_w"])
                load(arena[0:R, 1672:1673], ap["L0_ffn_enc_b"].rearrange("(r o) -> r o", o=1), slow=True)
                load(arena[0:NODES, 1680:1872], ap["L1_ffn_weights_in"])
                load(arena[0:E, 1872:2064], ap["L0_ffn_b2"])
                load(arena[:, 2064:2072], ap["L0_ffn_sw_b"].partition_broadcast(128))
                load(arena[0:KD, 2072:2084], ap["L1_attn_temperature"].rearrange("h a b -> (h a b)").partition_broadcast(KD))
                load(w_in[:, :, :], ap["L0_attn_w_in"].rearrange("(m p) n -> p m n", p=KD))
                load(w_norm[:, :], ap["L0_attn_w_norm"].rearrange("(m p) -> p m", p=KD), slow=True)
                load(conv_w[:, :, :], ap["L0_attn_conv_w"].rearrange("(m p) k -> p m k", p=128))
                load(conv_b[:, :], ap["L0_attn_conv_b"].rearrange("(m p) -> p m", p=128), slow=True)
                wx = ap["L0_attn_w_xproj"].rearrange("(m p) n -> p m n", p=128)
                load(w_x[:, :, 0:RANK], wx[:, :, 0:RANK])
                load(w_x[:, :, BROW:BROW + NS], wx[:, :, RANK:RANK + NS])
                load(w_x[:, :, CROW:CROW + NS], wx[:, :, RANK + NS:])
                load(w_dt[0:RANK, :], ap["L0_attn_w_dt"])
                load(b_dt[:, :], ap["L0_attn_b_dt"].rearrange("(m p) -> p m", p=128), slow=True)
                load(Aneg[:, :, :], ap["L0_attn_A_log"].rearrange("(m p) n -> p m n", p=128))
                load(Dp[:, :], ap["L0_attn_D_param"].rearrange("(m p) -> p m", p=128), slow=True)
                load(w_out[:, :, :], ap["L0_attn_w_out"].rearrange("(m p) n -> p m n", p=128))
                for k in range(2):
                    load(w_1[:, k, :].rearrange("p (e r) -> p e r", e=E),
                         ap["L0_ffn_w1"].rearrange("e (k p) r -> p k e r", p=KD)[:, k])
                load(b_1[:, :], ap["L0_ffn_b1"].rearrange("e r -> (e r)").rearrange("(m p) -> p m", p=128), slow=True)
                load(w_2[:, :, :], ap["L0_ffn_w2"].rearrange("e r n -> (e r) n").rearrange("(m p) n -> p m n", p=128))
                load(w_qkv[:, :, :], ap["L1_attn_w_qkv"].rearrange("(m p) n -> p m n", p=KD))
                load(w_pr[:, :, :], ap["L1_attn_w_proj"].rearrange("(m p) n -> p m n", p=KD))
                load(b_pr[:, :], ap["L1_attn_b_proj"].partition_broadcast(128))
                load(w_leaf[1:NODES, :], ap["L1_ffn_weights_out"][1:NODES, :])
                pos = ap["L0_tok_pos_embedding"][0]
                load(base[0:1, 0, :], ap["cls_tok"][0])
                load(base[1:128, 0, :], pos[0:127, :])
                load(base[:, 1:NT - 1, :], pos[127:127 + 128 * (NT - 2), :].rearrange("(j p) d -> p j d", p=128))
                load(base[0:LAST, NT - 1, :], pos[127 + 128 * (NT - 2):T - 1, :])
                for j in range(1, NT):
                    load(xt[:, j, :], ap["L0_tok_b"].partition_broadcast(128))
                load(xt[2:128, 0, :], ap["L0_tok_b"].partition_broadcast(126))
                load(xt[1:2, 0, :], ap["L0_tok_cls_token"][0])

            @block.gpsimd
            def _(g):
                g.sem_inc(out_stored, AHEAD["out_stored"])
                for k in range(SLOTS):
                    g.sem_inc(free[k], PSUM_AHEAD)
                g.memset(ident[:, :], 0.0).then_inc(s_setup_g, 1)
                g.wait_ge(s_setup_g, 1)
                g.affine_select(out=ident[:, :], in_=ident[:, :], compare_op=ALU.not_equal, fill=1.0,
                                base=0, pattern=[[-1, 128]], channel_multiplier=1).then_inc(s_setup_g, 1)
                g.wait_ge(s_setup_a, 1)
                v = self_w[:, :, :]
                g.affine_select(out=v, in_=v, compare_op=ALU.is_ge, fill=0.0, base=0,
                                pattern=[[KD, 2], [-DH, H]], channel_multiplier=1).then_inc(s_setup_g, 1)
                g.wait_ge(s_setup_g, 3)
                g.affine_select(out=v, in_=v, compare_op=ALU.is_ge, fill=0.0, base=DH - 1,
                                pattern=[[-KD, 2], [DH, H]], channel_multiplier=-1).then_inc(s_setup_g, 1)

            @block.vector
            def _(v):
                v.memset(arena[:, :], 0.0)
                v.memset(parts_f[:, :], 0.0)
                v.memset(qkf[:, :, :], 0.0)
                v.memset(xt[:, :, :], 0.0)
                v.memset(base[:, :, :], 0.0)
                v.memset(w_x[:, :, :], 0.0)
                v.memset(w_dt[:, :], 0.0)
                v.memset(ta[:, :, :], 1.0)
                v.memset(smid[:, :, :], 0.0)
                v.memset(w_leaf[:, :], 0.0).then_inc(s_setup_v, 1)
                for t, x in ((PS, 0.0), (ones, 1.0), (onesb, 1.0), (first15, 1.0), (clamp, CLAMP), (minus_half2, -0.5),
                             (prT, 0.0), (gated, 0.0), (xT, 0.0), (hotT, 0.0), (V, 0.0), 
                             (b_2, 0.0), (xin, 0.0), (shiftT, 0.0), (h, 0.0), (st, 0.0), (est, 0.0), (smax, 0.0)):
                    v.memset(t[tuple(slice(None) for _ in t.shape)], x).then_inc(s_setup_v, 1)
                for e in range(E):
                    v.memset(rank8[:, :, e], float(E - e)).then_inc(s_setup_v, 1)
                n = 1 + 18 + E
                v.wait_ge(s_setup_v, n)
                v.memset(first15[:, :].rearrange("p (a t) -> p a t", t=LS)[:, :, 0], 0.0)
                v.memset(V[:, :, :, DH:DH + 1], 1.0)
                v.wait_ge(s_w, n_w[0])
                for m in range(2):
                    v.tensor_scalar(w_in[:, m, :], w_in[:, m, :], w_norm[:, m:m + 1], None, ALU.mult)
                v.tensor_tensor(base[:, :, :], base[:, :, :], xt[:, :, :], ALU.add)
                for m in range(2):
                    src = arena[0:KD, 768 * m:768 * m + 768].rearrange("p (c a r e s) -> p a e c r s", c=C, a=2, r=8, e=2)
                    for a in range(2):
                        for e in range(2):
                            k = 2 * a + e
                            v.tensor_copy(wp[:, m, k, 0:128].rearrange("p (c r s) -> p c r s", c=2, r=8), src[:, a, e, 0:2])
                            ins = v.tensor_copy(wp2[:, m, k, :].rearrange("p (r s) -> p r s", r=8), src[:, a, e, 2])
                ins.then_inc(s_setup_v, 1)
                v.wait_ge(s_setup_v, n + 1)
                v.wait_ge(s_setup_g, 2)
                v.tensor_copy(identb[:, :], ident[:, :])
                v.tensor_scalar(negbig[:, :], ident[:, :], -BIG, None, ALU.mult)
                for k, row in enumerate((BROW, CROW)):
                    v.tensor_copy(sel_b[:, k, :], ident[0:KD, row:row + 1].to_broadcast([KD, 128]))
                for m in range(4):
                    for e in range(2):
                        v.tensor_copy(sel_e[:, m, R * e:R * e + R],
                                      ident[0:KD, 2 * m + e:2 * m + e + 1].to_broadcast([KD, R]))
                b2 = arena[0:E, 1872:2064]
                b2b = arena[0:E, 2100:2292]
                b2c = arena[0:E, 2292:2484]
                v.tensor_copy(b_2[0:E, 0, :], b2).then_inc(s_setup_v, 1)
                v.wait_ge(s_setup_v, n + 2)
                v.tensor_tensor(b2b, b2, b_2[0:E, 0, :], ALU.subtract).then_inc(s_setup_v, 1)
                v.wait_ge(s_setup_v, n + 3)
                v.tensor_copy(b_2[0:E, 1, :], b2b).then_inc(s_setup_v, 1)
                v.wait_ge(s_setup_v, n + 4)
                v.tensor_tensor(b2c, b2b, b_2[0:E, 1, :], ALU.subtract).then_inc(s_setup_v, 1)
                v.wait_ge(s_setup_v, n + 5)
                v.tensor_copy(b_2[0:E, 2, :], b2c).then_inc(s_setup_v, 1)
                v.wait_ge(s_setup_v, n + 6)
                v.wait_ge(s_setup_t, 1)
                v.tensor_copy(w_tok1[:, :, :].rearrange("p (b t) d -> p b (t d)", b=2), PS[:, 0:2, 0:2 * D])
                v.tensor_copy(w_tok2[:, :, :].rearrange("p t d -> p (t d)"), PS[:, 2, 0:2 * D])
                v.tensor_copy(arena[0:R, 2500:2500 + D], PS[0:R, 3, 0:D])
                v.tensor_copy(w_tree[:, :, :].rearrange("p m n -> p (m n)"), PS[0:KD, 4, 0:2 * NODES])
                v.tensor_copy(arena[0:R, 2700:2828], arena[0:R, 1672:1673].to_broadcast([R, 128])).then_inc(s_setup_v, 1)
                v.wait_ge(s_setup_t, 2)
                v.tensor_copy(w_route[:, :, :].rearrange("p m n -> p (m n)"), PS[0:KD, 5, 0:2 * E])
                v.tensor_tensor(b_route[:, :], arena[:, 2064:2072], PS[:, 6, 0:E], ALU.add)
                v.wait_ge(s_setup_a, 2)
                v.tensor_scalar(Aneg[:, :, :], Aneg[:, :, :], -1.0, None, ALU.mult).then_inc(s_setup_v, 1)

            @block.scalar
            def _(a):
                a.wait_ge(s_w, n_w[0])
                t_bc = arena[0:KD, 2072:2084]
                for m in range(2):
                    last = a.activation(self_w[:, m, :], t_bc, ACT.Copy, bias=0.25, scale=-0.25)
                last.then_inc(s_setup_a, 1)
                a.activation(Aneg[:, :, :], Aneg[:, :, :], ACT.Exp).then_inc(s_setup_a, 1)

            @block.tensor
            def _(t):
                t.wait_ge(s_w, n_w[0])
                t.wait_ge(s_setup_g, 2)
                t.wait_ge(s_setup_v, 1 + 18 + E + 1)
                for m in range(2):
                    for a in range(2):
                        for e in range(2):
                            t.transpose(PS[:, a, e * D + m * KD:e * D + (m + 1) * KD], wp[:, m, 2 * a + e, :],
                                        ident[0:KD, 0:KD])
                        t.transpose(PS[:, 2, a * D + m * KD:a * D + (m + 1) * KD],
                                    wp2[:, m, 2 * a:2 * a + 2, :].rearrange("p e x -> p (e x)"), ident[0:KD, 0:KD])
                    t.transpose(PS[0:R, 3, m * KD:(m + 1) * KD], arena[0:KD, 1536 + m * R:1536 + (m + 1) * R],
                                ident[0:KD, 0:KD])
                    last = t.transpose(PS[0:KD, 4, m * NODES:(m + 1) * NODES],
                                       arena[0:NODES, 1680 + m * KD:1680 + (m + 1) * KD], ident[0:NODES, 0:NODES])
                last.then_inc(s_setup_t, 1)
                t.wait_ge(s_setup_v, 1 + 18 + E + 1 + 5 + 1)
                for m in range(2):
                    t.matmul(PS[0:KD, 5, m * E:(m + 1) * E], lhsT=arena[0:R, 2500 + m * KD:2500 + (m + 1) * KD],
                             rhs=arena[0:R, 1664:1672], start=True, stop=True)
                t.matmul(PS[:, 6, 0:E], lhsT=arena[0:R, 2700:2828], rhs=arena[0:R, 1664:1672],
                         start=True, stop=True).then_inc(s_setup_t, 1)

        waits_apart = ctx.enter_context(nc.semaphore("waits_apart"))
        block = ctx.enter_context(nc.Block())

        def flat(job):
            return slot(job).rearrange("p b n -> p (b n)")

        def width(j):
            return LAST if j == NT - 1 else 128

        PARTS_Q = (0, 0, 1, 1, 0, 2)
        PARTS_K = (0, 1, 0, 1, 2, 0)

        @block.sync
        def _(sp):
            def heads_rows(w, part):
                return scr_qk[w, part].rearrange("(h d) c -> d h c", d=DH)

            sp.dma_start(xin[:, :, :].rearrange("y (c r) w -> y c r w", c=C),
                         ap["x"][0].rearrange("c (y r) w -> y c r w", r=8)).then_inc(pixels_in, 16)
            with sp.Fori(0, B) as i:
                sp.wait_ge(pixels_sorted, at(i, "pixels_sorted", 0))
                sp.dma_start(xin[:, :, :].rearrange("y (c r) w -> y c r w", c=C),
                             ap["x"][(i + 1) % B].rearrange("c (y r) w -> y c r w", r=8)).then_inc(pixels_in, 16)
                for w, parts_out in enumerate((q_parts_out, k_parts_out)):
                    sp.wait_ge(split_ready, at(i, "split_ready", 2 * w + 2))
                    for n in range(2):
                        sp.dma_start(scr_qk[w].rearrange("t (m p) c -> p t m c", p=KD)[:, :, n], parts[:, w, :, n]) \
                            .then_inc(parts_out, 16)
                sp.wait_ge(front_done, at(i, "front_done", 4))
                sp.wait_ge(q_parts_out, at(i, "q_parts_out", 32))
                for n, part in enumerate(PARTS_Q):
                    sp.dma_start(Qs[DH * n:DH * n + DH, 0:GH, :], heads_rows(0, part)[:, 0:GH]).then_inc(stack_in, 16)
                sp.wait_ge(k_parts_out, at(i, "k_parts_out", 32))
                for n, part in enumerate(PARTS_K):
                    sp.dma_start(Ks[DH * n:DH * n + DH, 0:GH, :], heads_rows(1, part)[:, 0:GH]).then_inc(stack_in, 16)
                for w, (dst, order) in enumerate(((Qs, PARTS_Q), (Ks, PARTS_K))):
                    for n, part in enumerate(order):
                        sp.dma_start(dst[DH * n:DH * n + DH, GH:H, :], heads_rows(w, part)[:, GH:H]) \
                            .then_inc(stack_rest_in, 16)
                for g in range(GROUPS):
                    sp.wait_ge(free[SLOT[f"shift{g}"]], freed(i, f"shift{g}"))
                    sp.dma_start(scr_shift[g], shiftT[:, g % 2, :]).then_inc(shift_out, 16)
                    sp.wait_ge(shift_out, at(i, "shift_out", 16 * (g + 1)))
                    sp.dma_start(Qs[KD:KD + 2, GH * g:GH * g + GH, :],
                                 scr_shift[g].rearrange("(n h) c -> n h c", n=2)).then_inc(shift_in, 16)
                sp.wait_ge(free[SLOT["out1"]], freed(i, "out1"))
                sp.dma_start(out[i, 0:128 * (NT - 1), :].rearrange("(j p) d -> p j d", p=128),
                             xt[:, 0:NT - 1, :]).then_inc(out_stored, 16)
                sp.dma_start(out[i, 128 * (NT - 1):T, :], xt[0:LAST, NT - 1, :]).then_inc(out_stored, 16)
            sp.wait_ge(out_stored, B * COUNTS["out_stored"] + AHEAD["out_stored"])

        @block.gpsimd
        def _(g):
            by_block = xin[:, :, :].rearrange("y r (x s) -> y r x s", s=8)

            def sort(px, r0, r1):
                for r in range(r0, r1, 8):
                    ins = g.tensor_scalar(px[:, :, 8 * (r - r0):8 * (r - r0) + 64].rearrange("y x (r s) -> y r x s", s=8),
                                          by_block[:, r:r + 8], 1.0, 0.0, ALU.mult, ALU.add)
                return ins

            def embedded_deviations():
                g.tensor_scalar(ers[:, 2, :], emv[:, :, 1], EPS, None, ALU.add)
                return g.tensor_scalar(ers[:, 3, :], emv[:, :, 1], 1.0 + EPS, EPS * EPS, ALU.mult, ALU.add)

            g.wait_ge(pixels_in, 16)
            g.sem_inc(waits_apart, 1)
            sort(px2, 16, 24).then_inc(pixels_sorted, 1)
            sort(px1, 0, 16).then_inc(pixels_sorted, 1)
            g.wait_ge(emb_stats_ready, 1)
            g.sem_inc(waits_apart, 1)
            embedded_deviations().then_inc(first_emb, 1)
            g.wait_ge(first_emb, 1)
            g.tensor_tensor(ers[:, 0:2, :], ers[:, 2:4, :], minus_half2[:, :, :], ALU.pow).then_inc(emb_rstd_ready, 1)
            with g.Fori(0, B) as i:
                links = [0]

                def link(ins):
                    links[0] += 1
                    ins.then_inc(pool_chain, 1)
                    g.wait_ge(pool_chain, at(i, "pool_chain", links[0]))

                for k in range(4):
                    if k > 0:
                        g.wait_ge(stats_ready, at(i, "stats_ready", k))
                        g.sem_inc(waits_apart, 1)
                        link(g.tensor_scalar(rs[:, 1, :], mv[:, :, 1], EPS, None, ALU.add))
                        g.tensor_tensor(rs[:, 0, :], rs[:, 1, :], minus_half[:, :], ALU.pow).then_inc(rstd_ready, 1)
                        g.wait_ge(rstd_ready, at(i, "rstd_ready", k))
                    if k == 0:
                        g.wait_ge(norm_ready, at(i, "norm_ready", NT * 1))
                        g.tensor_tensor(h[:, :, :], h[:, :, :], emb[:, :, :], ALU.add).then_inc(h_summed, 1)

                        def times_gate(m):
                            g.tensor_tensor(cz[:, m, :], Cs, zs[:, m, 0:T2], ALU.mult).then_inc(cz_ready, 1)

                        g.wait_ge(h_summed, at(i, "h_summed", 1))
                        g.wait_ge(c_rows_taken, at(i, "c_rows_taken", 1))
                        times_gate(0)
                        times_gate(1)
                        for m in range(ND):
                            g.wait_ge(delta_ready, at(i, "delta_ready", m + 1))
                            link(g.tensor_tensor(du[:, m, 0:T2], dl[:, m, 0:T2], u[:, m, 0:T2], ALU.mult))
                            if m == 0:
                                g.wait_ge(free[SLOT["B0"]], freed(i, "B0"))
                            g.tensor_tensor(gated[:, m, 0:T2], du[:, m, 0:T2], Bs, ALU.mult).then_inc(du_ready, 1)
                        times_gate(2)
                        for m in range(ND):
                            g.wait_ge(ud_ready, at(i, "ud_ready", m + 1))
                            g.tensor_tensor(u[:, m, 0:T2], u[:, m, 0:T2], zs[:, m, 0:T2], ALU.mult).then_inc(udz_ready, 1)
                        g.wait_ge(end_ready, at(i, "end_ready", 1))
                        g.sem_inc(waits_apart, 1)
                        g.partition_all_reduce(alive[:, 1:2], alive[:, 0:1], 128, bass.bass_isa.ReduceOp.max).then_inc(alive_ready, 1)
                    if k == 1:
                        g.wait_ge(pixels_in, at(i, "pixels_in", 16))
                        g.wait_ge(gated_ready, at(i, "gated_ready", 1))
                        g.sem_inc(waits_apart, 1)
                        sort(px2, 16, 24).then_inc(pixels_sorted, 1)
                        sort(px1, 0, 16).then_inc(pixels_sorted, 1)
                    if k == 2:
                        g.wait_ge(norm_ready, at(i, "norm_ready", NT * 3))
                        g.tensor_tensor(h[:, :, :], h[:, :, :],
                                        b_pr[:, :].unsqueeze(1).to_broadcast([128, NT, D]), ALU.add).then_inc(h_summed, 1)
                        g.wait_ge(h_summed, at(i, "h_summed", 2))
                        g.sem_inc(waits_apart, 1)
                        g.memset(Ks[KD:KD + 2, :, :], 1.0).then_inc(ones_ready, 1)
                g.wait_ge(emb_stats_ready, at(i, "emb_stats_ready", 1))
                g.sem_inc(waits_apart, 1)
                link(embedded_deviations())
                g.tensor_tensor(ers[:, 0:2, :], ers[:, 2:4, :], minus_half2[:, :, :], ALU.pow).then_inc(emb_rstd_ready, 1)
                assert links[0] == COUNTS["pool_chain"], links

        @block.scalar
        def _(a):
            def take_blocks(n):
                dst, nx = (bl2, 14 - n % 2) if n < 2 else (bl1, 14)
                x0 = 14 * (n % 2)
                return a.activation(dst[:, :, x0:x0 + nx].rearrange("p y x -> p x y"),
                                    ACC[:, n % 2, 0:nx * NY].rearrange("p (x y) -> p x y", y=NY), ACT.Copy)

            def take_patches(n):
                m, c = divmod(n, 2)
                rows_y = 14 - c
                return a.activation(tokT[:, m, 2 + 14 * OUT * c:2 + 14 * OUT * c + rows_y * OUT],
                                    ACC[0:KD, c, 0:rows_y * OUT], ACT.Copy)

            for n in range(4):
                a.wait_ge(front_done, n + 1)
                take_blocks(n).then_inc(front_taken, 1)
            for n in range(4):
                a.wait_ge(front_done, n + 5)
                take_patches(n).then_inc(front_taken, 1)
            with a.Fori(0, B) as i:
                def load_table(k, func):
                    a.activation(warm[:, k:k + 1], ones[:, 0:1], func)

                def transposed(name):
                    for m in range(2):
                        a.wait_ge(full[SLOT[f"{name}{m}"]], filled(i, f"{name}{m}"))
                        a.activation(xT[:, m, :], flat(f"{name}{m}")[0:KD, 0:TW], ACT.Copy).then_inc(free[SLOT[f"{name}{m}"]], 1)

                transposed("xnT")
                for m in range(ND):
                    a.wait_ge(full[SLOT[f"xz{m}"]], filled(i, f"xz{m}"))
                    ins = a.activation(xi[:, m, 3:3 + T2].rearrange("p (b t) -> p b t", b=2), wide(f"xz{m}"), ACT.Copy)
                    ins.then_inc(free[SLOT[f"xz{m}"]], 1)
                for m in range(ND):
                    a.wait_ge(full[SLOT[f"xz{ND + m}"]], filled(i, f"xz{ND + m}"))
                    ins = a.activation(zs[:, m, 0:T2].rearrange("p (b t) -> p b t", b=2), wide(f"xz{ND + m}"), ACT.Silu)
                    ins.then_inc(free[SLOT[f"xz{ND + m}"]], 1)
                for m in range(ND):
                    a.wait_ge(conv_ready, at(i, "conv_ready", m + 1))
                    a.activation(u[:, m, 0:T2], gated[:, m, 0:T2], ACT.Silu).then_inc(u_ready, 1)
                a.wait_ge(full[SLOT["proj"]], filled(i, "proj"))
                a.activation(prT[:, 0:T2].rearrange("p (b t) -> p b t", b=2), wide("proj", KD), ACT.Copy).then_inc(free[SLOT["proj"]], 1)
                load_table(0, ACT.Exp)
                for m in range(ND):
                    a.wait_ge(pre_ready, at(i, "pre_ready", m + 1))
                    ins = a.activation(dl[:, m, 0:T2], dl[:, m, 0:T2], ACT.Exp)
                ins.then_inc(exp3_ready, 1)
                a.wait_ge(c_rows_ready, at(i, "c_rows_ready", 1))
                a.activation(Cs.rearrange("p (b t) -> p b t", b=2), ACC[:, :, 0:CW], ACT.Copy).then_inc(c_rows_taken, 1)
                a.wait_ge(exp3_ready, at(i, "exp3_ready", 1))
                for m in range(ND):
                    a.activation(dl[:, m, 0:T2], dl[:, m, 0:T2], ACT.Ln, bias=1.0).then_inc(soft_ready, 1)
                a.wait_ge(h_summed, at(i, "h_summed", 1))
                a.wait_ge(full[SLOT["B0"]], filled(i, "B0"))
                a.activation(Bs.rearrange("p (b t) -> p b t", b=2), wide("B0"), ACT.Copy).then_inc(free[SLOT["B0"]], 1)
                load_table(1, ACT.Exp)
                for m in range(ND):
                    a.wait_ge(decay_log_ready, at(i, "decay_log_ready", m + 1))
                    a.activation(gg[:, m, 0:T2], gg[:, m, 0:T2], ACT.Exp)
                    a.activation(lw[:, m, 0:T2], lw[:, m, 0:T2], ACT.Exp, bias=clamp[:, :]).then_inc(decays_ready, 1)
                a.wait_ge(log15_ready, at(i, "log15_ready", 1))
                a.activation(g15, g15, ACT.Exp)
                a.activation(s15, l15, ACT.Exp, bias=clamp[:, :]).then_inc(decays15_ready, 1)
                for m in range(ND):
                    a.wait_ge(du_ready, at(i, "du_ready", m + 1))
                    a.activation(u[:, m, 0:T2], u[:, m, 0:T2], ACT.Copy, scale=Dp[:, m:m + 1]).then_inc(ud_ready, 1)
                a.wait_ge(tail_flag, at(i, "tail_flag", 1))
                a.sem_inc(waits_apart, 1)
                with a.If(a.value_load(flag[0:1, 0:1]) != 0):
                    with a.Fori(0, NG) as n:
                        for m in range(ND):
                            a.wait_ge(tail_log, i * COUNTS["tail_log"] + n * ND + (m + 1))
                            a.activation(gg[:, m, LS:T2], gg[:, m, LS:T2], ACT.Exp)
                            a.activation(lw[:, m, LS:T2], lw[:, m, LS:T2], ACT.Exp, bias=clamp[:, :]) \
                                .then_inc(tail_exp, 1)
                with a.Else():
                    a.sem_inc(tail_exp, COUNTS["tail_exp"])

                transposed("x2T")
                load_table(2, ACT.Exp)
                a.wait_ge(logits_ready, at(i, "logits_ready", 1))
                a.activation(logit[:, :, :], hot[:, :, :], ACT.Exp).then_inc(exp_ready, 1)
                for m in range(4):
                    if m == 2:
                        a.wait_ge(full[SLOT["hotT"]], filled(i, "hotT"))
                        a.activation(hotT[0:E, :], flat("hotT")[0:E, 0:TW], ACT.Copy).then_inc(free[SLOT["hotT"]], 1)
                    a.wait_ge(full[SLOT[f"hid{m}"]], filled(i, f"hid{m}"))
                    ins = a.activation(gated[:, m, 0:T2].rearrange("p (b t) -> p b t", b=2), wide(f"hid{m}"), ACT.Gelu,
                                       bias=b_1[:, m:m + 1])
                    ins.then_inc(free[SLOT[f"hid{m}"]], 1)
                for n in range(4):
                    a.wait_ge(front_done, at(i, "front_done", n + 1))
                    take_blocks(n).then_inc(front_taken, 1)

                transposed("x3T")
                for w in range(2):
                    for n in (2 * w, 2 * w + 1):
                        job = ("q0", "q1", "k0", "k1")[n]
                        a.wait_ge(full[SLOT[job]], filled(i, job))
                        ins = a.activation(qkf[0:KD, n, :].rearrange("p (b t) -> p b t", b=2), wide(job, KD), ACT.Copy,
                                           scale=DH ** -0.5 if w == 0 else 1.0)
                        ins.then_inc(free[SLOT[job]], 1)
                        a.wait_ge(free[SLOT[job]], freed(i, job))
                        a.activation(parts[:, w, 0, n % 2, :], qkf[0:KD, n, :], ACT.Copy).then_inc(parts1_ready, 1)
                    for n in (2 * w, 2 * w + 1):
                        a.wait_ge(rest_ready, at(i, "rest_ready", n + 1))
                        a.activation(parts[:, w, 1, n % 2, :], rest[0:KD, n, :], ACT.Copy).then_inc(parts2_ready, 1)
                for q, (j0, nj) in enumerate(HALVES):
                    a.wait_ge(full[SLOT[f"v{q}"]], filled(i, f"v{q}"))
                    nb = nj // 2
                    a.activation(V[:, j0:j0 + nj, :, 0:DH].rearrange("p (b j) h d -> p b (j h) d", b=nb),
                                            slot(f"v{q}")[:, 0:nb, 0:2 * D].rearrange("p b (x d) -> p b x d", d=DH),
                                            ACT.Copy).then_inc(free[SLOT[f"v{q}"]], 1)
                a.activation(tokT[:, :, 0:2], ident[0:KD, 124:128].rearrange("p (m c) -> p m c", m=2), ACT.Copy)
                for n in range(4):
                    a.wait_ge(front_done, at(i, "front_done", n + 5))
                    take_patches(n).then_inc(front_taken, 1)

                def take_shift(g):
                    if g == 2:
                        a.wait_ge(shift_out, at(i, "shift_out", 16))
                    a.wait_ge(full[SLOT[f"shift{g}"]], filled(i, f"shift{g}"))
                    a.activation(shiftT[:, g % 2, :], flat(f"shift{g}")[0:2 * GH, 0:T2], ACT.Copy) \
                        .then_inc(free[SLOT[f"shift{g}"]], 1)
                    a.wait_ge(shift_ready, at(i, "shift_ready", g + 1))
                    a.activation(sself[:, :, GH * g:GH * g + GH], smid[:, :, GH * g:GH * g + GH], ACT.Exp) \
                        .then_inc(self_exp, 1)
                take_shift(0)
                for n in range(STEPS):
                    g, j = divmod(n, NT)
                    if n >= 2:
                        a.wait_ge(pv_done, at(i, "pv_done", n - 1))
                    for hh in range(GH):
                        job = f"ST{GH * g + hh}_{j}"
                        w = width(j)
                        a.wait_ge(full[SLOT[job]], filled(i, job))
                        ins = a.activation(PT[0:w, GH * (n % 2) + hh, :].rearrange("p (b t) -> p b t", b=2),
                                           wide(job, w), ACT.Exp)
                        ins.then_inc(free[SLOT[job]], 1)
                    if n in SHIFT_AT:
                        take_shift(SHIFT_AT[n])
                for m in range(2):
                    a.wait_ge(full[SLOT[f"aoT{m}"]], filled(i, f"aoT{m}"))
                    a.activation(xT[:, m, :], flat(f"aoT{m}")[0:KD, 0:TW], ACT.Copy).then_inc(free[SLOT[f"aoT{m}"]], 1)

                transposed("x4T")
                load_table(3, ACT.Gelu)
                a.wait_ge(tree_ready, at(i, "tree_ready", 1))
                a.activation(te[:, :, :], tl[:, :, :], ACT.Gelu).then_inc(tree_gelu, 1)
                a.wait_ge(full[SLOT["coefT"]], filled(i, "coefT"))
                a.activation(coefT[0:NODES, :], flat("coefT")[0:NODES, 0:TW], ACT.Copy).then_inc(free[SLOT["coefT"]], 1)

        @block.vector
        def _(v):
            def embed(q, src):
                j0, nj = HALVES[q]
                j1 = j0 + nj
                return v.tensor_tensor(emb[:, j0:j1, :].rearrange("p (b j) d -> p b (j d)", j=2),
                                       src[:, 0:nj // 2, 0:2 * D],
                                       base[:, j0:j1, :].rearrange("p (b j) d -> p b (j d)", j=2), ALU.add)

            def embedded_stats(q):
                j0, nj = HALVES[q]
                for j in range(j0, j0 + nj):
                    ins = v.bn_stats(est[:, j, :], emb[:, j, :])
                return ins

            def embedded_moments():
                for j in range(NT):
                    ins = v.bn_aggr(emv[:, j, :], est[:, j, :])
                return ins

            for q in range(2):
                v.wait_ge(first_emb_full, q + 1)
                embed(q, PS[:, 2 * q:2 * q + 2, :]).then_inc(first_emb_read, 1)
                v.wait_ge(first_emb_read, q + 1)
                ins = embedded_stats(q)
            ins.then_inc(first_emb_read, 1)
            v.wait_ge(first_emb_read, 3)
            v.sem_inc(waits_apart, 1)
            embedded_moments().then_inc(emb_stats_ready, 1)
            with v.Fori(0, B) as i:
                links = [0]

                def link(ins):
                    links[0] += 1
                    ins.then_inc(dve_chain, 1)
                    v.wait_ge(dve_chain, at(i, "dve_chain", links[0]))


                def pairs(job, nj):
                    return slot(job)[:, 0:nj // 2, 0:2 * D]

                def tiles(x, j0, nj):
                    return x[:, j0:j0 + nj, :].rearrange("p (b j) d -> p b (j d)", j=2)

                def layernorm(k):
                    for j in range(NT):
                        ins = v.bn_aggr(mv[:, j, :], st[:, j, :])
                    ins.then_inc(stats_ready, 1)
                    v.wait_ge(stats_ready, at(i, "stats_ready", k))
                    v.wait_ge(rstd_ready, at(i, "rstd_ready", k))
                    if k == 1:
                        v.wait_ge(out_stored, at(i, "out_stored", 0))
                        v.sem_inc(waits_apart, 1)
                    for j in range(NT):
                        v.tensor_scalar(xt[:, j, :], h[:, j, :], mv[:, j, 0:1], rs[:, 0, j:j + 1],
                                        ALU.subtract, ALU.mult).then_inc(norm_ready, 1)
                    v.wait_ge(norm_ready, at(i, "norm_ready", NT * (k + 1)))

                def stats(j0, nj):
                    for j in range(j0, j0 + nj):
                        ins = v.bn_stats(st[:, j, :], h[:, j, :])
                    if j0 > 0:
                        link(ins)
                        v.sem_inc(waits_apart, 1)

                def add_to_h(name, src=h, dst=h):
                    for q, (j0, nj) in enumerate(HALVES):
                        v.wait_ge(full[SLOT[f"{name}{q}"]], filled(i, f"{name}{q}"))
                        ins = v.tensor_tensor(tiles(dst, j0, nj), pairs(f"{name}{q}", nj), tiles(src, j0, nj), ALU.add)
                        ins.then_inc(free[SLOT[f"{name}{q}"]], 1)
                        v.wait_ge(free[SLOT[f"{name}{q}"]], freed(i, f"{name}{q}"))
                        if dst is h:
                            v.sem_inc(waits_apart, 1)
                            stats(j0, nj)

                v.wait_ge(emb_rstd_ready, at(i, "emb_rstd_ready", 0))
                for dst, r, ready in ((xn, 1, xn_ready), (h, 0, norm_ready)):
                    for j in range(NT):
                        v.tensor_scalar(dst[:, j, :], emb[:, j, :], emv[:, j, 0:1], ers[:, r, j:j + 1],
                                        ALU.subtract, ALU.mult).then_inc(ready, 1)

                v.wait_ge(free[SLOT["xz0"]], freed(i, "xz0"))
                link(v.memset(xi[:, :, 0:3], 0.0))
                for m in range(ND):
                    v.wait_ge(free[SLOT[f"xz{m}"]], freed(i, f"xz{m}"))
                    yc = gated[:, m, 0:T2]
                    link(v.tensor_scalar(yc, xi[:, m, 0:T2], conv_w[:, m, 0:1], conv_b[:, m:m + 1], ALU.mult, ALU.add))
                    for k in range(1, 4):
                        ins = v.scalar_tensor_tensor(yc, xi[:, m, k:k + T2], conv_w[:, m, k:k + 1], yc, ALU.mult, ALU.add)
                        if k < 3:
                            link(ins)
                    ins.then_inc(conv_ready, 1)

                def halves(x):
                    return x.rearrange("p (b t) -> p b t", b=2)
                for m in range(ND):
                    v.wait_ge(full[SLOT[f"dt{m}"]], filled(i, f"dt{m}"))
                    v.tensor_scalar(halves(dl[:, m, 0:T2]), wide(f"dt{m}"), b_dt[:, m:m + 1], 40.0,
                                              ALU.add, ALU.min).then_inc(pre_ready, 1)
                for m in range(ND):
                    v.wait_ge(soft_ready, at(i, "soft_ready", m + 1))
                    v.scalar_tensor_tensor(halves(dl[:, m, 0:T2]), wide(f"dt{m}"), b_dt[:, m:m + 1],
                                                      halves(dl[:, m, 0:T2]), ALU.add, ALU.max).then_inc(free[SLOT[f"dt{m}"]], 1)
                    v.wait_ge(free[SLOT[f"dt{m}"]], freed(i, f"dt{m}"))
                    v.tensor_scalar(gg[:, m, 0:T2], dl[:, m, 0:T2], Aneg[:, m, 0:1], LOW,
                                                   ALU.mult, ALU.max).then_inc(delta_ready, 1)
                    v.wait_ge(delta_ready, at(i, "delta_ready", m + 1))
                    v.tensor_tensor_scan(lw[:, m, 0:T2], onesb[:, :], gg[:, m, 0:T2], 0.0,
                                                   ALU.mult, ALU.add).then_inc(decay_log_ready, 1)
                v.wait_ge(free[SLOT["proj"]], freed(i, "proj"))
                for row, bd in ((BROW, bdB), (CROW, bdC)):
                    ins = v.tensor_tensor(bd.rearrange("p (n t) -> p n t", t=LS),
                                          prT[:, 0:LS].unsqueeze(1).to_broadcast([KD, NG, LS]),
                                          ident[0:KD, row + 1:row + NS].unsqueeze(2).to_broadcast([KD, NG, LS]), ALU.mult)
                ins.then_inc(bc_ready, 1)

                def by_state(x):
                    return x.rearrange("p (m n t) -> p m n t", m=ND, n=NG)
                for m in range(ND):
                    ins = v.tensor_tensor(by_state(g15)[:, m], dl[:, m, 0:LS].unsqueeze(1).to_broadcast([128, NG, LS]),
                                          Aneg[:, m, 1:NS].unsqueeze(2).to_broadcast([128, NG, LS]), ALU.mult)
                link(ins)
                link(v.tensor_scalar(g15, g15, LOW, None, ALU.max))
                v.tensor_tensor_scan(l15, first15[:, :], g15, 0.0, ALU.mult, ALU.add).then_inc(log15_ready, 1)

                for m in range(ND):
                    y = gated[:, m, 0:T2]
                    v.wait_ge(decays_ready, at(i, "decays_ready", m + 1))
                    v.wait_ge(du_ready, at(i, "du_ready", m + 1))
                    link(v.scalar_tensor_tensor(lw[:, m, 0:T2], lw[:, m, 0:T2], 1.0, y, ALU.min, ALU.mult))
                    link(v.tensor_tensor_scan(gg[:, m, 0:T2], gg[:, m, 0:T2], lw[:, m, 0:T2], 0.0, ALU.mult, ALU.add))
                    v.wait_ge(cz_ready, at(i, "cz_ready", m + 1))
                    ins = v.tensor_tensor(y, gg[:, m, 0:T2], cz[:, m, :], ALU.mult)
                link(ins)

                v.wait_ge(full[SLOT["BC15"]], filled(i, "BC15"))
                v.wait_ge(decays15_ready, at(i, "decays15_ready", 1))
                v.memset(by_state(g15)[:, :, :, 0], 0.0)
                v.tensor_copy(ends15[:, 0], by_state(l15)[:, :, :, LS - 1])
                v.tensor_reduce(alive[:, 0:1], by_state(l15)[:, :, :, LS - 1], AX.XY, ALU.max).then_inc(end_ready, 1)
                B15 = slot("BC15")[:, 0, 0:NG * LS].rearrange("p (n t) -> p n t", t=LS)
                C15 = slot("BC15")[:, 1, 0:NG * LS].rearrange("p (n t) -> p n t", t=LS)
                for m in range(ND):
                    ins = v.tensor_tensor(by_state(x15)[:, m], du[:, m, 0:LS].unsqueeze(1).to_broadcast([128, NG, LS]),
                                          B15, ALU.mult)
                link(ins)
                link(v.scalar_tensor_tensor(x15, s15, 1.0, x15, ALU.min, ALU.mult))
                link(v.tensor_tensor_scan(s15, g15, x15, 0.0, ALU.mult, ALU.add))
                v.tensor_copy(ends15[:, 1], by_state(s15)[:, :, :, LS - 1])
                for m in range(ND):
                    ins = v.tensor_tensor(by_state(x15)[:, m], by_state(s15)[:, m], C15, ALU.mult)
                ins.then_inc(free[SLOT["BC15"]], 1)
                v.wait_ge(free[SLOT["BC15"]], freed(i, "BC15"))
                y15 = g15[:, 0:ND * LS].rearrange("p (m t) -> p m t", m=ND)
                for m in range(ND):
                    ins = v.tensor_reduce(y15[:, m], by_state(x15)[:, m].rearrange("p n t -> p t n"), AX.X, ALU.add)
                link(ins)
                link(v.tensor_tensor(y15, y15, zs[:, :, 0:LS], ALU.mult))
                v.tensor_tensor(gated[:, 0:ND, 0:LS], gated[:, 0:ND, 0:LS], y15, ALU.add).then_inc(gated15_ready, 1)
                v.wait_ge(alive_ready, at(i, "alive_ready", 1))
                v.tensor_scalar(flag[0:1, :], alive[0:1, 1:2], DEAD, None, ALU.is_gt).then_inc(tail_flag, 1)
                v.wait_ge(tail_flag, at(i, "tail_flag", 1))
                v.sem_inc(waits_apart, 1)
                with v.If(v.value_load(flag[0:1, 0:1]) != 0):
                    with v.Fori(0, NG) as n:
                        steps = [0]

                        def tail_link(ins):
                            steps[0] += 1
                            ins.then_inc(tail_chain, 1)
                            v.wait_ge(tail_chain, i * COUNTS["tail_chain"] + n * TAIL_STEPS + steps[0])
                        for m in range(ND):
                            tail_link(v.tensor_scalar(gg[:, m, LS:T2], dl[:, m, LS:T2], Aneg[:, m, bass.ds(n + 1, 1)], LOW,
                                                      ALU.mult, ALU.max))
                            v.tensor_tensor_scan(lw[:, m, LS:T2], onesb[:, LS:T2], gg[:, m, LS:T2],
                                                 ends15[:, 0, m, bass.ds(n, 1)], ALU.mult, ALU.add).then_inc(tail_log, 1)
                        v.wait_ge(tail_bc, i * COUNTS["tail_bc"] + n + 1)
                        x = gated[:, ND, 0:T2]
                        for m in range(ND):
                            v.wait_ge(tail_exp, i * COUNTS["tail_exp"] + n * ND + (m + 1))
                            tail_link(v.tensor_tensor(halves(x), halves(du[:, m, 0:T2]), ACC[:, :, 0:CW], ALU.mult))
                            tail_link(v.scalar_tensor_tensor(lw[:, m, LS:T2], lw[:, m, LS:T2], 1.0, x[:, LS:T2],
                                                             ALU.min, ALU.mult))
                            tail_link(v.tensor_tensor_scan(gg[:, m, LS:T2], gg[:, m, LS:T2], lw[:, m, LS:T2],
                                                           ends15[:, 1, m, bass.ds(n, 1)], ALU.mult, ALU.add))
                            tail_link(v.tensor_tensor(halves(x), halves(gg[:, m, 0:T2]), wide("BC15"), ALU.mult))
                            tail_link(v.tensor_tensor(x, x, zs[:, m, 0:T2], ALU.mult))
                            ins = v.tensor_tensor(gated[:, m, LS:T2], gated[:, m, LS:T2], x[:, LS:T2], ALU.add)
                            if m < ND - 1:
                                tail_link(ins)
                            else:
                                ins.then_inc(tail_used, 1)
                                v.wait_ge(tail_used, i * COUNTS["tail_used"] + n + 1)
                        assert steps[0] == TAIL_STEPS, steps
                with v.Else():
                    v.sem_inc(tail_log, COUNTS["tail_log"])
                    v.sem_inc(tail_used, COUNTS["tail_used"])
                    v.sem_inc(tail_chain, COUNTS["tail_chain"])

                v.wait_ge(gated15_ready, at(i, "gated15_ready", 1))
                v.sem_inc(gated_ready, 1)
                v.wait_ge(h_summed, at(i, "h_summed", 1))
                add_to_h("mix")

                layernorm(1)
                v.wait_ge(full[SLOT["route"]], filled(i, "route"))
                ins = v.tensor_tensor(logit[:, :, :], slot("route")[:, 0, 0:NT * E].rearrange("p (j e) -> p j e", e=E),
                                      b_route[:, :].unsqueeze(1).to_broadcast([128, NT, E]), ALU.add)
                ins.then_inc(free[SLOT["route"]], 1)
                v.wait_ge(free[SLOT["route"]], freed(i, "route"))
                link(v.tensor_reduce(best[:, 0, :], logit[:, :, :], AX.X, ALU.max))
                v.tensor_tensor(hot[:, :, :], logit[:, :, :], best[:, 0, :].unsqueeze(2).to_broadcast([128, NT, E]),
                                          ALU.subtract).then_inc(logits_ready, 1)
                v.wait_ge(exp_ready, at(i, "exp_ready", 1))
                link(v.tensor_reduce(best[:, 1, :], logit[:, :, :], AX.X, ALU.add))
                link(v.reciprocal(best[:, 3, :], best[:, 1, :]))
                link(v.scalar_tensor_tensor(hot[:, :, :].rearrange("p j e -> p (j e)"),
                                               hot[:, :, :].rearrange("p j e -> p (j e)"), 0.0,
                                               rank8[:, :, :].rearrange("p j e -> p (j e)"), ALU.is_equal, ALU.mult))
                link(v.tensor_reduce(best[:, 2, :], hot[:, :, :], AX.X, ALU.max))
                v.tensor_tensor(hot[:, :, :], hot[:, :, :], best[:, 2, :].unsqueeze(2).to_broadcast([128, NT, E]),
                                          ALU.is_equal).then_inc(hot_ready, 1)
                for m in range(4):
                    v.wait_ge(full[SLOT[f"mask{m}"]], filled(i, f"mask{m}"))
                    v.wait_ge(free[SLOT[f"hid{m}"]], freed(i, f"hid{m}"))
                    v.tensor_tensor(halves(gated[:, m, 0:T2]), wide(f"mask{m}"), halves(gated[:, m, 0:T2]),
                                               ALU.mult).then_inc(free[SLOT[f"mask{m}"]], 1)
                for q, (j0, nj) in enumerate(HALVES):
                    v.wait_ge(full[SLOT[f"ffn{q}"]], filled(i, f"ffn{q}"))
                    for j in range(nj):
                        ins = v.scalar_tensor_tensor(h[:, j0 + j, :], slot(f"ffn{q}")[:, j // 2, D * (j % 2):D * (j % 2) + D],
                                                     best[:, 3, j0 + j:j0 + j + 1], h[:, j0 + j, :], ALU.mult, ALU.add)
                    ins.then_inc(free[SLOT[f"ffn{q}"]], 1)
                    v.wait_ge(free[SLOT[f"ffn{q}"]], freed(i, f"ffn{q}"))
                    v.sem_inc(waits_apart, 1)
                    stats(j0, nj)

                layernorm(2)
                for w in range(2):
                    for n in (2 * w, 2 * w + 1):
                        v.wait_ge(parts1_ready, at(i, "parts1_ready", n + 1))
                        v.tensor_tensor(rest[0:KD, n, :], qkf[0:KD, n, :], parts[:, w, 0, n % 2, :],
                                        ALU.subtract).then_inc(rest_ready, 1)
                    for n in (2 * w, 2 * w + 1):
                        v.wait_ge(parts2_ready, at(i, "parts2_ready", n + 1))
                        v.tensor_tensor(parts[:, w, 2, n % 2, :], rest[0:KD, n, :], parts[:, w, 1, n % 2, :],
                                        ALU.subtract).then_inc(split_ready, 1)
                for m in range(2):
                    v.tensor_tensor(prod[0:KD, 4 + m, :], qkf[0:KD, m, :], qkf[0:KD, 2 + m, :], ALU.mult) \
                        .then_inc(selfprod_ready, 1)
                v.wait_ge(full[SLOT["self"]], filled(i, "self"))
                sv = slot("self")[:, 0, 0:NT * H].rearrange("p (j h) -> p j h", h=H)
                v.tensor_copy(smid[:, 0:NT - 1, :], sv[:, 0:NT - 1])
                v.tensor_copy(smid[0:LAST, NT - 1, :], sv[0:LAST, NT - 1]).then_inc(free[SLOT["self"]], 1)
                v.wait_ge(free[SLOT["self"]], freed(i, "self"))

                def take_output(g):
                    v.wait_ge(pv_done, at(i, "pv_done", NT * (g + 1)))
                    v.tensor_copy(halves(OT[:, g, 0:T2]), ACC[:, :, 0:CW]).then_inc(pv_taken, 1)

                def finish_heads(g):
                    heads = slice(GH * g, GH * g + GH)
                    job = f"oT{g}"
                    v.wait_ge(full[SLOT[job]], filled(i, job))
                    v.wait_ge(self_exp, at(i, "self_exp", g + 1))
                    o_all = flat(job)[:, 0:TW].rearrange("p (j h d) -> p j h d", h=GH, d=32)
                    for j0, j1, w in ((0, NT - 1, 128), (NT - 1, NT, LAST)):
                        o = o_all[0:w, j0:j1]
                        dn = den[0:w, j0:j1, :]
                        ao = xt[0:w, j0:j1, :].rearrange("p j (h d) -> p j h d", d=DH)[:, :, heads]
                        shape = [w, j1 - j0, GH, DH]
                        v.tensor_tensor(dn, o[:, :, :, DH], sself[0:w, j0:j1, heads], ALU.add)
                        link(v.tensor_tensor(ao, V[0:w, j0:j1, heads, 0:DH],
                                             sself[0:w, j0:j1, heads].unsqueeze(3).to_broadcast(shape), ALU.mult))
                        v.reciprocal(dn, dn)
                        ins = v.tensor_tensor(ao, o[:, :, :, 0:DH], ao, ALU.add)
                        if j1 == NT:
                            ins.then_inc(free[SLOT[job]], 1)
                            v.wait_ge(free[SLOT[job]], freed(i, job))
                        else:
                            link(ins)
                        ins = v.tensor_tensor(ao, ao, dn.unsqueeze(3).to_broadcast(shape), ALU.mult)
                    ins.then_inc(ao_ready, 1)

                for s in range(S_JOBS):
                    hd, j = divmod(s, NT)
                    job = f"S{hd}_{j}"
                    w = width(j)
                    if s == OT_TAKEN_AT:
                        take_output(0)
                    v.wait_ge(full[SLOT[job]], filled(i, job))
                    v.tensor_reduce(smax[0:w, hd, j:j + 1], wide(job, w), AX.XY, ALU.max).then_inc(free[SLOT[job]], 1)
                    if s % S_GROUP == S_GROUP - 1:
                        g = s // S_GROUP
                        heads = slice(GH * g, GH * g + GH)
                        part1, part2 = shift[:, :, g, 0:GH], shift[:, :, g, GH:2 * GH]
                        v.wait_ge(free[SLOT[job]], freed(i, job))
                        link(v.tensor_tensor(stot[:, :, heads], smax[:, heads, :].rearrange("p h j -> p j h"),
                                             smid[:, :, heads], ALU.max))
                        link(v.tensor_scalar(stot[:, :, heads], stot[:, :, heads], -1.0, None, ALU.mult))
                        link(v.tensor_copy(mb[:, 0, :, heads], stot[:, :, heads]))
                        link(v.tensor_copy(part1, mb[:, 0, :, heads]))
                        link(v.tensor_tensor(stot[:, :, heads], stot[:, :, heads], part1, ALU.subtract))
                        link(v.tensor_copy(mb[:, 1, :, heads], stot[:, :, heads]))
                        link(v.tensor_copy(part2, mb[:, 1, :, heads]))
                        link(v.tensor_tensor(stot[:, :, heads], part1, part2, ALU.add))
                        v.tensor_tensor(smid[:, :, heads], smid[:, :, heads], stot[:, :, heads], ALU.add) \
                            .then_inc(shift_ready, 1)
                finish_heads(0)
                take_output(1)
                finish_heads(1)
                take_output(2)
                finish_heads(2)
                v.wait_ge(h_summed, at(i, "h_summed", 2))
                add_to_h("att")

                layernorm(3)
                v.wait_ge(full[SLOT["tree"]], filled(i, "tree"))
                ins = v.tensor_copy(tl[:, :, :], slot("tree")[:, 0, 0:NT * NODES].rearrange("p (j n) -> p j n", n=NODES))
                ins.then_inc(free[SLOT["tree"]], 1)
                v.wait_ge(free[SLOT["tree"]], freed(i, "tree"))
                v.tensor_scalar(tc[:, :, :], tl[:, :, :], 0.0, None, ALU.is_gt).then_inc(tree_ready, 1)
                v.wait_ge(tree_ready, at(i, "tree_ready", 1))
                v.tensor_copy(ta[:, :, 2], tc[:, :, 0])
                link(v.tensor_scalar(ta[:, :, 1], tc[:, :, 0], -1.0, 1.0, ALU.mult, ALU.add))
                for a0, a1 in ((1, 3), (3, 7), (7, 10)):
                    right = ta[:, :, 2 * a0 + 2:2 * a1 + 1:2]
                    link(v.tensor_tensor(right, ta[:, :, a0:a1], tc[:, :, a0:a1], ALU.mult))
                    link(v.tensor_tensor(ta[:, :, 2 * a0 + 1:2 * a1:2], ta[:, :, a0:a1], right, ALU.subtract))
                link(v.tensor_reduce(tsum[:, :], ta[:, :, 10:15], AX.X, ALU.add))
                link(v.tensor_tensor(ta[:, :, 20], ta[:, :, 20], tsum[:, :], ALU.add))
                v.wait_ge(tree_gelu, at(i, "tree_gelu", 1))
                link(v.tensor_tensor(tl[:, :, :], ta[:, :, :], te[:, :, :], ALU.mult))
                link(v.tensor_tensor(tc[:, :, 0:10], tc[:, :, 0:10], tl[:, :, 0:10], ALU.mult))
                v.tensor_copy(cf[:, :, 2:21:2], tc[:, :, 0:10])
                v.tensor_tensor(cf[:, :, 1:20:2], tl[:, :, 0:10], tc[:, :, 0:10], ALU.subtract)
                v.memset(cf[:, :, 0], 0.0)
                link(v.tensor_reduce(tsum[:, :], tl[:, :, 10:21], AX.X, ALU.add))
                link(v.tensor_tensor(cf[:, :, 20], cf[:, :, 20], tsum[:, :], ALU.add))
                v.scalar_tensor_tensor(cf[:, :, 20], te[:, :, 20], float(DEPTH - 1 - 5), cf[:, :, 20], ALU.mult, ALU.add).then_inc(coef_ready, 1)
                for q in range(2):
                    v.wait_ge(full[SLOT[f"emb{q}"]], filled(i, f"emb{q}"))
                    embed(q, slot(f"emb{q}")).then_inc(free[SLOT[f"emb{q}"]], 1)
                    v.wait_ge(free[SLOT[f"emb{q}"]], freed(i, f"emb{q}"))
                    v.sem_inc(waits_apart, 1)
                    ins = embedded_stats(q)
                link(ins)
                v.sem_inc(waits_apart, 1)
                embedded_moments().then_inc(emb_stats_ready, 1)
                v.wait_ge(emb_stats_ready, at(i, "emb_stats_ready", 1))
                add_to_h("out", h, xt)
                assert links[0] == COUNTS["dve_chain"], links

        @block.tensor
        def _(t):
            def transpose_blocks(n):
                for x in range(14 * (n % 2), 14 * (n % 2) + (13 if n == 1 else 14)):
                    src = px1[:, x, :] if n >= 2 else px2[:, x:x + 2, :].rearrange("y e n -> y (e n)")
                    ins = t.transpose(ACC[:, n % 2, NY * (x % 14):NY * (x % 14) + NY], src, ident[0:NY, 0:NY])
                return ins

            TAPS = 6

            def patch_product(n, tap):
                m, c = divmod(n, 2)
                y0, ny = 14 * c, 14 - c
                o = ACC[0:KD, c, 0:ny * OUT].rearrange("p (y x) -> p y x", x=OUT)
                cols = slice(KD * m, KD * m + KD)
                if tap < 4:
                    a, e = divmod(tap, 2)
                    return t.matmul(o, lhsT=w_tok1[:, tap, cols], rhs=bl1[:, y0 + a:y0 + a + ny, e:e + OUT],
                                    start=tap == 0, stop=False)
                a = tap - 4
                return t.matmul(o, lhsT=w_tok2[:, a, cols], rhs=bl2[:, y0 + a:y0 + a + ny, 0:OUT],
                                start=False, stop=tap == TAPS - 1)

            t.wait_ge(pixels_sorted, 2)
            for n in range(4):
                if n >= 2:
                    t.wait_ge(front_taken, n - 1)
                    t.sem_inc(waits_apart, 1)
                transpose_blocks(n).then_inc(front_done, 1)
            t.wait_ge(front_taken, 4)
            for n in range(4):
                if n >= 2:
                    t.wait_ge(front_taken, n + 3)
                for tap in range(TAPS):
                    ins = patch_product(n, tap)
                ins.then_inc(front_done, 1)
            t.wait_ge(front_taken, 8)

            def embedded_tokens(q, dst):
                j0, nj = HALVES[q]
                for m in range(2):
                    for j in range(nj):
                        ins = t.transpose(dst[:, j // 2, D * (j % 2) + KD * m:D * (j % 2) + KD * m + KD],
                                          tokT[:, m, 128 * (j0 + j):128 * (j0 + j) + 128], ident[0:KD, 0:KD])
                return ins

            for q in range(2):
                embedded_tokens(q, PS[:, 2 * q:2 * q + 2, :]).then_inc(first_emb_full, 1)
            t.wait_ge(first_emb_read, 2)
            with t.Fori(0, B) as i:

                def feature_major(job, n, terms):
                    t.wait_ge(free[SLOT[job]], vacant(i, job))
                    for c in range(2):
                        for k, (lhsT, rhs) in enumerate(terms):
                            ins = t.matmul(slot(job)[0:n, c, 0:CW], lhsT=lhsT, rhs=rhs[:, c * CW:(c + 1) * CW],
                                           start=k == 0, stop=k == len(terms) - 1)
                    ins.then_inc(full[SLOT[job]], 1)

                def token_major(job, j0, nj, terms):
                    t.wait_ge(free[SLOT[job]], vacant(i, job))
                    for j in range(nj):
                        for k, (lhsT, rhs) in enumerate(terms):
                            ins = t.matmul(slot(job)[:, j // 2, D * (j % 2):D * (j % 2) + D],
                                           lhsT=lhsT[:, 128 * (j0 + j):128 * (j0 + j) + 128], rhs=rhs,
                                           start=k == 0, stop=k == len(terms) - 1)
                    ins.then_inc(full[SLOT[job]], 1)

                def transposes(name, src, norm=None):
                    for m in range(2):
                        t.wait_ge(free[SLOT[f"{name}{m}"]], vacant(i, f"{name}{m}"))
                        for j in range(NT):
                            if norm == 0 and m == 0:
                                t.wait_ge(xn_ready, at(i, "xn_ready", j + 1))
                                t.sem_inc(waits_apart, 1)
                            elif norm and m == 0:
                                t.wait_ge(norm_ready, at(i, "norm_ready", NT * norm + j + 1))
                                t.sem_inc(waits_apart, 1)
                            ins = t.transpose(flat(f"{name}{m}")[0:KD, 128 * j:128 * j + 128],
                                              src[:, j, KD * m:KD * m + KD], ident[:, :])
                        ins.then_inc(full[SLOT[f"{name}{m}"]], 1)

                def half_ready(name):
                    t.wait_ge(free[SLOT[f"{name}0"]], freed(i, f"{name}0"))
                    t.wait_ge(free[SLOT[f"{name}1"]], freed(i, f"{name}1"))

                def mix_product(q, j, rows_m, m, start, stop):
                    j1 = HALVES[q][0] + j
                    return t.matmul(slot(f"mix{q}")[:, j // 2, D * (j % 2):D * (j % 2) + D],
                                    lhsT=rows_m[:, 128 * j1:128 * j1 + 128], rhs=w_out[:, m, :], start=start, stop=stop)

                transposes("xnT", xn, 0)
                half_ready("xnT")
                for m in range(2 * ND):
                    feature_major(f"xz{m}", 128, [(w_in[:, k, 128 * m:128 * m + 128], xT[:, k, :]) for k in range(2)])
                t.wait_ge(u_ready, at(i, "u_ready", 3))
                feature_major("proj", KD, [(w_x[:, m, :], u[:, m, :]) for m in range(ND)])
                t.wait_ge(free[SLOT["proj"]], freed(i, "proj"))
                for m in range(ND):
                    feature_major(f"dt{m}", 128, [(w_dt[:, 128 * m:128 * m + 128], prT[:, :])])
                for c in range(2):
                    ins = t.matmul(ACC[:, c, 0:CW], lhsT=sel_b[:, 1, :], rhs=prT[:, c * CW:(c + 1) * CW],
                                   start=True, stop=True)
                ins.then_inc(c_rows_ready, 1)
                feature_major("B0", 128, [(sel_b[:, 0, :], prT[:, :])])
                t.wait_ge(bc_ready, at(i, "bc_ready", 1))
                t.wait_ge(free[SLOT["BC15"]], vacant(i, "BC15"))
                for k, bd in enumerate((bdB, bdC)):
                    ins = t.matmul(slot("BC15")[:, k, 0:NG * LS], lhsT=ones[0:KD, 0:128], rhs=bd, start=True, stop=True)
                ins.then_inc(full[SLOT["BC15"]], 1)
                for q, (j0, nj) in enumerate(HALVES):
                    t.wait_ge(free[SLOT[f"mix{q}"]], vacant(i, f"mix{q}"))
                    for m in range(ND):
                        if q == 0:
                            t.wait_ge(udz_ready, at(i, "udz_ready", m + 1))
                        for j in range(nj):
                            mix_product(q, j, u[:, m, :], m, m == 0 and j % 2 == 0, False)
                t.wait_ge(tail_flag, at(i, "tail_flag", 1))
                t.sem_inc(waits_apart, 1)
                with t.If(t.value_load(flag[0:1, 0:1]) != 0):
                    for n in range(NG):
                        if n > 0:
                            t.wait_ge(tail_used, at(i, "tail_used", n))
                        for banks, row in ((ACC, BROW + 1 + n), (slot("BC15"), CROW + 1 + n)):
                            for c in range(2):
                                ins = t.matmul(banks[:, c, 0:CW], lhsT=ident[0:KD, row:row + 1].to_broadcast([KD, 128]),
                                               rhs=prT[:, c * CW:(c + 1) * CW], start=True, stop=True)
                        ins.then_inc(tail_bc, 1)
                with t.Else():
                    t.sem_inc(tail_bc, COUNTS["tail_bc"])
                t.wait_ge(gated_ready, at(i, "gated_ready", 1))
                for q, (j0, nj) in enumerate(HALVES):
                    for m in range(ND):
                        for j in range(nj):
                            ins = mix_product(q, j, gated[:, m, :], m, False, m == ND - 1 and j % 2 == 1)
                    ins.then_inc(full[SLOT[f"mix{q}"]], 1)

                transposes("x2T", xt, 1)
                half_ready("x2T")
                t.wait_ge(free[SLOT["route"]], vacant(i, "route"))
                for j in range(NT):
                    for m in range(2):
                        ins = t.matmul(slot("route")[:, 0, E * j:E * j + E], lhsT=xT[:, m, 128 * j:128 * j + 128],
                                       rhs=w_route[:, m, :], start=m == 0, stop=m == 1)
                ins.then_inc(full[SLOT["route"]], 1)
                def hidden(m):
                    feature_major(f"hid{m}", 128, [(w_1[:, k, 128 * m:128 * m + 128], xT[:, k, :]) for k in range(2)])

                hidden(0)
                hidden(1)
                t.wait_ge(hot_ready, at(i, "hot_ready", 1))
                t.wait_ge(free[SLOT["hotT"]], vacant(i, "hotT"))
                for j in range(NT):
                    ins = t.transpose(flat("hotT")[0:E, 128 * j:128 * j + 128], hot[:, j, :], ident[:, :])
                ins.then_inc(full[SLOT["hotT"]], 1)
                hidden(2)
                t.wait_ge(free[SLOT["hotT"]], freed(i, "hotT"))
                for m in range(2):
                    feature_major(f"mask{m}", 128, [(sel_e[:, m, :], hotT[:, :])])
                hidden(3)
                for m in (2, 3):
                    feature_major(f"mask{m}", 128, [(sel_e[:, m, :], hotT[:, :])])
                for n in range(2):
                    t.wait_ge(pixels_sorted, at(i, "pixels_sorted", 1))
                    t.sem_inc(waits_apart, 1)
                    transpose_blocks(n).then_inc(front_done, 1)
                for m in range(4):
                    t.wait_ge(free[SLOT[f"mask{m}"]], freed(i, f"mask{m}"))
                for q, (j0, nj) in enumerate(HALVES):
                    token_major(f"ffn{q}", j0, nj, [(gated[:, m, :], w_2[:, m, :]) for m in range(4)]
                                + [(hotT[:, :], b_2[:, k, :]) for k in range(3)])

                for n in (2, 3):
                    t.wait_ge(pixels_sorted, at(i, "pixels_sorted", 2))
                    t.wait_ge(front_taken, at(i, "front_taken", n - 1))
                    t.sem_inc(waits_apart, 1)
                    transpose_blocks(n).then_inc(front_done, 1)
                transposes("x3T", xt, 2)
                half_ready("x3T")
                for k, job in enumerate(("q0", "q1", "k0", "k1")):
                    feature_major(job, KD, [(w_qkv[:, n, KD * k:KD * k + KD], xT[:, n, :]) for n in range(2)])
                for q, (j0, nj) in enumerate(HALVES):
                    token_major(f"v{q}", j0, nj, [(xT[:, n, :], w_qkv[:, n, 2 * D:3 * D]) for n in range(2)])
                for n in range(2):
                    t.wait_ge(front_taken, at(i, "front_taken", 4))
                    for tap in range(TAPS):
                        ins = patch_product(n, tap)
                    ins.then_inc(front_done, 1)

                t.wait_ge(selfprod_ready, at(i, "selfprod_ready", 2))
                t.wait_ge(free[SLOT["self"]], vacant(i, "self"))
                for j in range(NT):
                    w = width(j)
                    for m in range(2):
                        ins = t.matmul(slot("self")[0:w, 0, H * j:H * j + H], lhsT=prod[0:KD, 4 + m, 128 * j:128 * j + w],
                                       rhs=self_w[:, m, :], start=m == 0, stop=m == 1)
                ins.then_inc(full[SLOT["self"]], 1)

                def without_diagonal(job, w, j, starts, n_rows, left, right):
                    t.wait_ge(free[SLOT[job]], vacant(i, job))
                    for c, c0 in enumerate(starts):
                        lo, hi = max(128 * j, c0), min(128 * j + w, c0 + CW)
                        t_ins = t.matmul(slot(job)[0:w, c, 0:CW], lhsT=left[0:n_rows, 128 * j:128 * j + w],
                                         rhs=right[0:n_rows, c0:c0 + CW], start=True, stop=lo >= hi)
                        if lo < hi:
                            t_ins = t.matmul(slot(job)[0:w, c, lo - c0:hi - c0], lhsT=identb[0:w, 0:w],
                                             rhs=negbig[0:w, lo - 128 * j:hi - 128 * j], start=False, stop=True)
                    t_ins.then_inc(full[SLOT[job]], 1)

                def maxima_product(s):
                    hd, j = divmod(s, NT)
                    without_diagonal(f"S{hd}_{j}", width(j), j, (0, T - CW), KD, Qs[:, hd, :], Ks[:, hd, :])

                def shift_rows(g):
                    t.wait_ge(shift_ready, at(i, "shift_ready", g + 1))
                    t.wait_ge(free[SLOT[f"shift{g}"]], vacant(i, f"shift{g}"))
                    for j in range(NT):
                        ins = t.transpose(flat(f"shift{g}")[0:2 * GH, 128 * j:128 * j + 128], shift[:, j, g, :], ident[:, :])
                    ins.then_inc(full[SLOT[f"shift{g}"]], 1)

                def weigh(n, c):
                    g, j = divmod(n, NT)
                    w = width(j)
                    if c == 0:
                        if j == 0 and g > 0:
                            t.wait_ge(pv_taken, at(i, "pv_taken", g))
                        if n == 0:
                            t.wait_ge(front_taken, at(i, "front_taken", 8))
                        last_job = f"ST{GH * g + GH - 1}_{j}"
                        t.wait_ge(free[SLOT[last_job]], freed(i, last_job))
                    for hh in range(GH):
                        ins = t.matmul(ACC[32 * hh:32 * hh + 32, c, 0:CW], lhsT=V[0:w, j, GH * g + hh, :],
                                       rhs=PT[0:w, GH * (n % 2) + hh, c * CW:(c + 1) * CW],
                                       start=j == 0, stop=j == NT - 1, tile_position=(0, 32 * hh))
                    if c == 1:
                        ins.then_inc(pv_done, 1)

                def output_tokens(g):
                    t.wait_ge(pv_taken, at(i, "pv_taken", g + 1))
                    t.wait_ge(free[SLOT[f"oT{g}"]], vacant(i, f"oT{g}"))
                    for j in range(NT):
                        ins = t.transpose(flat(f"oT{g}")[:, 128 * j:128 * j + 128], OT[:, g, 128 * j:128 * j + 128], ident[:, :])
                    ins.then_inc(full[SLOT[f"oT{g}"]], 1)

                t.wait_ge(stack_in, at(i, "stack_in", 192))
                for s in range(SHIFT0_AT):
                    if s == S_GROUP:
                        t.wait_ge(stack_rest_in, at(i, "stack_rest_in", 192))
                    maxima_product(s)
                    if s % 2 == 1 and s // 2 < 2 * TAPS:
                        n, tap = divmod(s // 2, TAPS)
                        if tap == 0:
                            t.wait_ge(front_taken, at(i, "front_taken", n + 5))
                        ins = patch_product(n + 2, tap)
                        if tap == TAPS - 1:
                            ins.then_inc(front_done, 1)
                shift_rows(0)
                for s in range(SHIFT0_AT, S_FIRST):
                    maxima_product(s)
                t.wait_ge(ones_ready, at(i, "ones_ready", 1))
                s = S_FIRST
                for n in range(STEPS):
                    g, j = divmod(n, NT)
                    if j == 0:
                        t.wait_ge(shift_in, at(i, "shift_in", 16 * (g + 1)))
                    for hd in range(GH * g, GH * g + GH):
                        without_diagonal(f"ST{hd}_{j}", width(j), j, (0, CW), KD + 2, Ks[:, hd, :], Qs[:, hd, :])
                        if s < S_JOBS:
                            maxima_product(s)
                            s += 1
                        if n > 0 and hd % 2 == 1:
                            weigh(n - 1, hd % GH // 2)
                    if n in SHIFT_AT:
                        shift_rows(SHIFT_AT[n])
                    if n in OT_AT:
                        output_tokens(OT_AT[n])
                for c in range(2):
                    weigh(STEPS - 1, c)
                output_tokens(2)
                t.wait_ge(ao_ready, at(i, "ao_ready", 3))
                transposes("aoT", xt)
                half_ready("aoT")
                for q, (j0, nj) in enumerate(HALVES):
                    token_major(f"att{q}", j0, nj, [(xT[:, k, :], w_pr[:, k, :]) for k in range(2)])

                transposes("x4T", xt, 3)
                half_ready("x4T")
                t.wait_ge(free[SLOT["tree"]], vacant(i, "tree"))
                for j in range(NT):
                    for m in range(2):
                        ins = t.matmul(slot("tree")[:, 0, NODES * j:NODES * j + NODES], lhsT=xT[:, m, 128 * j:128 * j + 128],
                                       rhs=w_tree[:, m, :], start=m == 0, stop=m == 1)
                ins.then_inc(full[SLOT["tree"]], 1)
                for q in range(2):
                    t.wait_ge(free[SLOT[f"emb{q}"]], vacant(i, f"emb{q}"))
                    embedded_tokens(q, slot(f"emb{q}")).then_inc(full[SLOT[f"emb{q}"]], 1)
                t.wait_ge(coef_ready, at(i, "coef_ready", 1))
                t.wait_ge(free[SLOT["coefT"]], vacant(i, "coefT"))
                for j in range(NT):
                    ins = t.transpose(flat("coefT")[0:NODES, 128 * j:128 * j + 128], cf[:, j, :], ident[:, :])
                ins.then_inc(full[SLOT["coefT"]], 1)
                t.wait_ge(free[SLOT["coefT"]], freed(i, "coefT"))
                for q, (j0, nj) in enumerate(HALVES):
                    token_major(f"out{q}", j0, nj, [(coefT[:, :], w_leaf[:, :])])



_INS = ["x", "cls_tok", "L0_tok_w", "L0_tok_b", "L0_tok_cls_token", "L0_tok_pos_embedding", "L0_attn_w_norm",
        "L0_attn_w_in", "L0_attn_conv_w", "L0_attn_conv_b", "L0_attn_w_xproj", "L0_attn_w_dt", "L0_attn_b_dt",
        "L0_attn_A_log", "L0_attn_D_param", "L0_attn_w_out", "L0_ffn_enc_w", "L0_ffn_enc_b", "L0_ffn_sw_w",
        "L0_ffn_sw_b", "L0_ffn_w1", "L0_ffn_b1", "L0_ffn_w2", "L0_ffn_b2", "L1_attn_w_qkv", "L1_attn_w_proj",
        "L1_attn_b_proj", "L1_attn_temperature", "L1_ffn_weights_in", "L1_ffn_weights_out"]


def kernel(**inputs):
    import concourse.bacc as bacc
    from concourse.bass_utils import run_bass_kernel_spmd

    nc = bacc.Bacc("TRN2", target_bir_lowering=False, num_devices=1)
    arrays, ap = {}, {}
    for name in _INS:
        a = np.ascontiguousarray(inputs[name])
        arrays[f"in_{name}"] = a
        ap[name] = nc.dram_tensor(f"in_{name}", a.shape, mybir.dt.from_np(a.dtype), kind="ExternalInput").ap()
    out = nc.dram_tensor("out", (B, T, D), F32, kind="ExternalOutput").ap()
    tower(nc, ap, out)
    return run_bass_kernel_spmd(nc, [arrays], core_ids=[0]).results[0]["out"]
```
